# Optimizing a Trainium2 kernel written in Bass

```python
import numpy as np
import jax
import jax.numpy as jnp

def _softmax(x, axis=-1):
    return jax.nn.softmax(x, axis=axis)

def _gelu(x):
    return jax.nn.gelu(x, approximate=True)

def _silu(x):
    return jax.nn.silu(x)

def _sigmoid(x):
    return jax.nn.sigmoid(x)

def _layernorm(x, axis=-1, eps=1e-05):
    m = jnp.mean(x, axis=axis, keepdims=True)
    v = jnp.var(x, axis=axis, keepdims=True)
    return (x - m) / jnp.sqrt(v + eps)

def _scatter_add(tgt, idx, src, axis=0):
    return tgt.at[idx].add(src)

def _segment_sum(src, seg, n):
    return jax.ops.segment_sum(src, seg, n)
kernel_name = 'mk_hybrid_d1_jaxref_r8_7aa3c0'

def setup_inputs(seed: int=0):
    np.random.seed(seed)
    _w = jnp.asarray

    def _L0_attn_a_setup():
        import jax, jax.numpy as jnp
        import numpy as np
        key = jax.random.key(seed)
        ks = jax.random.split(key, 5)
        B, T, C = (2, 256, 128)
        x = jax.random.normal(ks[0], (B, T, C), dtype=jnp.float32)
        Wqkv = jax.random.normal(ks[1], (C, 3 * C), dtype=jnp.float32) * C ** (-0.5)
        bqkv = jax.random.normal(ks[2], (3 * C,), dtype=jnp.float32) * 0.02
        Wproj = jax.random.normal(ks[3], (C, C), dtype=jnp.float32) * C ** (-0.5)
        bproj = jax.random.normal(ks[4], (C,), dtype=jnp.float32) * 0.02
        return {'x': x, 'Wqkv': Wqkv, 'bqkv': bqkv, 'Wproj': Wproj, 'bproj': bproj}
    _L0_attn_a_in = _L0_attn_a_setup()

    def _L0_attn_b_setup():
        import jax, jax.numpy as jnp
        import numpy as np
        DIM = 128
        D_STATE = 32
        HEADDIM = 64
        EXPAND = 2
        CHUNK = 64
        D_INNER = EXPAND * DIM
        NHEADS = D_INNER // HEADDIM
        ROPE_DIM = int(0.5 * D_STATE)
        D_IN_PROJ = 2 * D_INNER + 2 * D_STATE + NHEADS
        B_SZ = 4
        L = 512

        def _segsum(a):
            T = a.shape[-1]
            cs = jnp.cumsum(a, axis=-1)
            d = cs[..., :, None] - cs[..., None, :]
            mask = jnp.tril(jnp.ones((T, T), bool))
            return jnp.where(mask, d, -jnp.inf)

        def _rope(v):
            t = jnp.arange(v.shape[1], dtype=jnp.float32)
            inv_freq = 1.0 / 10000.0 ** (jnp.arange(0, ROPE_DIM, 2, dtype=jnp.float32) / ROPE_DIM)
            ang = t[:, None] * inv_freq[None, :]
            cos, sin = (jnp.cos(ang)[None], jnp.sin(ang)[None])
            vr, vp = (v[..., :ROPE_DIM], v[..., ROPE_DIM:])
            v1, v2 = (vr[..., 0::2], vr[..., 1::2])
            r = jnp.stack([v1 * cos - v2 * sin, v1 * sin + v2 * cos], axis=-1)
            return jnp.concatenate([r.reshape(vr.shape), vp], axis=-1)
        key = jax.random.key(seed)
        ks = jax.random.split(key, 8)
        return {'x': jax.random.normal(ks[0], (B_SZ, L, DIM), jnp.float32), 'ln_w': jnp.ones((DIM,), jnp.float32), 'ln_b': jnp.zeros((DIM,), jnp.float32), 'W_in': jax.random.normal(ks[1], (DIM, D_IN_PROJ), jnp.float32) * 0.02, 'dt_bias': jax.random.uniform(ks[2], (NHEADS,), jnp.float32, -4.0, -1.0), 'A_log': jnp.log(jax.random.uniform(ks[3], (NHEADS,), jnp.float32, 1.0, 16.0)), 'D': jax.random.normal(ks[4], (NHEADS,), jnp.float32) * 0.1 + 1.0, 'rms_w': jnp.ones((D_INNER,), jnp.float32), 'W_out': jax.random.normal(ks[5], (D_INNER, DIM), jnp.float32) * 0.02}
    _L0_attn_b_in = _L0_attn_b_setup()

    def _L0_ffn_setup():
        import jax, jax.numpy as jnp
        import numpy as np
        D_MODEL = 128
        N_HEADS = 16
        HEAD_DIM = D_MODEL // N_HEADS
        KV_LATENT = 64
        N_EXPERTS = 4
        D_HIDDEN = 4 * D_MODEL
        B, T = (2, 128)

        def rmsnorm(x, w, eps=1e-06):
            return w * (x * jax.lax.rsqrt(jnp.mean(x * x, axis=-1, keepdims=True) + eps))

        def layernorm(x, g, b, eps=1e-05):
            mu = jnp.mean(x, axis=-1, keepdims=True)
            var = jnp.mean((x - mu) ** 2, axis=-1, keepdims=True)
            return (x - mu) * jax.lax.rsqrt(var + eps) * g + b

        def apply_rope(x):
            t, d = (x.shape[2], x.shape[3])
            half = d // 2
            pos = jnp.arange(t, dtype=x.dtype)[:, None]
            inv_freq = 1.0 / 10000.0 ** (jnp.arange(half, dtype=x.dtype) / half)
            ang = pos * inv_freq[None, :]
            sin, cos = (jnp.sin(ang), jnp.cos(ang))
            x1, x2 = (x[..., :half], x[..., half:])
            return jnp.concatenate([x1 * cos - x2 * sin, x1 * sin + x2 * cos], axis=-1)

        def mla_attention(x, Wq, Wdkv, Wuk, Wuv, Wo, ln_g, ln_b):
            b, t, _ = x.shape
            q = (x @ Wq.T).reshape(b, t, N_HEADS, HEAD_DIM).transpose(0, 2, 1, 3)
            latent = layernorm(x @ Wdkv.T, ln_g, ln_b)
            k = (latent @ Wuk.T).reshape(b, t, N_HEADS, HEAD_DIM).transpose(0, 2, 1, 3)
            v = (latent @ Wuv.T).reshape(b, t, N_HEADS, HEAD_DIM).transpose(0, 2, 1, 3)
            q = apply_rope(q)
            k = apply_rope(k)
            scores = jnp.einsum('bhqd,bhkd->bhqk', q, k) / np.sqrt(HEAD_DIM)
            causal = jnp.tril(jnp.ones((t, t), dtype=bool))
            scores = jnp.where(causal, scores, -jnp.inf)
            attn = jax.nn.softmax(scores, axis=-1)
            out = jnp.einsum('bhqk,bhkd->bhqd', attn, v).transpose(0, 2, 1, 3).reshape(b, t, D_MODEL)
            return out @ Wo.T

        def moe(x, gate_w, gate_b, W1, b1, W2, b2):
            logits = x @ gate_w.T + gate_b
            top = jnp.argmax(logits, axis=-1)
            onehot = jax.nn.one_hot(top, N_EXPERTS, dtype=x.dtype)
            h = jax.nn.relu(jnp.einsum('btd,ehd->bteh', x, W1) + b1)
            y = jnp.einsum('bteh,edh->bted', h, W2) + b2
            return jnp.einsum('bted,bte->btd', y, onehot)
        key = jax.random.key(seed)
        ks = jax.random.split(key, 16)
        s = lambda fan_in: 1.0 / np.sqrt(fan_in)
        return {'x': jax.random.normal(ks[0], (B, T, D_MODEL), jnp.float32), 'norm1_w': jnp.ones((D_MODEL,), jnp.float32), 'norm2_w': jnp.ones((D_MODEL,), jnp.float32), 'Wq': jax.random.normal(ks[1], (D_MODEL, D_MODEL), jnp.float32) * s(D_MODEL), 'Wdkv': jax.random.normal(ks[2], (KV_LATENT, D_MODEL), jnp.float32) * s(D_MODEL), 'Wuk': jax.random.normal(ks[3], (D_MODEL, KV_LATENT), jnp.float32) * s(KV_LATENT), 'Wuv': jax.random.normal(ks[4], (D_MODEL, KV_LATENT), jnp.float32) * s(KV_LATENT), 'Wo': jax.random.normal(ks[5], (D_MODEL, D_MODEL), jnp.float32) * s(D_MODEL), 'ln_g': jnp.ones((KV_LATENT,), jnp.float32), 'ln_b': jnp.zeros((KV_LATENT,), jnp.float32), 'gate_w': jax.random.normal(ks[6], (N_EXPERTS, D_MODEL), jnp.float32) * s(D_MODEL), 'gate_b': jnp.zeros((N_EXPERTS,), jnp.float32), 'W1': jax.random.normal(ks[7], (N_EXPERTS, D_HIDDEN, D_MODEL), jnp.float32) * s(D_MODEL), 'b1': jnp.zeros((N_EXPERTS, D_HIDDEN), jnp.float32), 'W2': jax.random.normal(ks[8], (N_EXPERTS, D_MODEL, D_HIDDEN), jnp.float32) * s(D_HIDDEN), 'b2': jnp.zeros((N_EXPERTS, D_MODEL), jnp.float32)}
    _L0_ffn_in = _L0_ffn_setup()
    _d = {'L0_attn_a_x': _L0_attn_a_in['x'], 'L0_attn_a_Wqkv': _L0_attn_a_in['Wqkv'], 'L0_attn_a_bqkv': _L0_attn_a_in['bqkv'], 'L0_attn_a_Wproj': _L0_attn_a_in['Wproj'], 'L0_attn_a_bproj': _L0_attn_a_in['bproj'], 'L0_attn_b_ln_w': _L0_attn_b_in['ln_w'], 'L0_attn_b_ln_b': _L0_attn_b_in['ln_b'], 'L0_attn_b_W_in': _L0_attn_b_in['W_in'], 'L0_attn_b_dt_bias': _L0_attn_b_in['dt_bias'], 'L0_attn_b_A_log': _L0_attn_b_in['A_log'], 'L0_attn_b_D': _L0_attn_b_in['D'], 'L0_attn_b_rms_w': _L0_attn_b_in['rms_w'], 'L0_attn_b_W_out': _L0_attn_b_in['W_out'], 'L0_ffn_norm1_w': _L0_ffn_in['norm1_w'], 'L0_ffn_norm2_w': _L0_ffn_in['norm2_w'], 'L0_ffn_Wq': _L0_ffn_in['Wq'], 'L0_ffn_Wdkv': _L0_ffn_in['Wdkv'], 'L0_ffn_Wuk': _L0_ffn_in['Wuk'], 'L0_ffn_Wuv': _L0_ffn_in['Wuv'], 'L0_ffn_Wo': _L0_ffn_in['Wo'], 'L0_ffn_ln_g': _L0_ffn_in['ln_g'], 'L0_ffn_ln_b': _L0_ffn_in['ln_b'], 'L0_ffn_gate_w': _L0_ffn_in['gate_w'], 'L0_ffn_gate_b': _L0_ffn_in['gate_b'], 'L0_ffn_W1': _L0_ffn_in['W1'], 'L0_ffn_b1': _L0_ffn_in['b1'], 'L0_ffn_W2': _L0_ffn_in['W2'], 'L0_ffn_b2': _L0_ffn_in['b2']}
    _x0 = _d['L0_attn_a_x']
    _d['L0_attn_a_x'] = jax.random.normal(jax.random.fold_in(jax.random.key(seed), 1), (16, 256, 128), dtype=_x0.dtype)
    del _x0
    return _d

def reference(L0_attn_a_x, L0_attn_a_Wqkv, L0_attn_a_bqkv, L0_attn_a_Wproj, L0_attn_a_bproj, L0_attn_b_ln_w, L0_attn_b_ln_b, L0_attn_b_W_in, L0_attn_b_dt_bias, L0_attn_b_A_log, L0_attn_b_D, L0_attn_b_rms_w, L0_attn_b_W_out, L0_ffn_norm1_w, L0_ffn_norm2_w, L0_ffn_Wq, L0_ffn_Wdkv, L0_ffn_Wuk, L0_ffn_Wuv, L0_ffn_Wo, L0_ffn_ln_g, L0_ffn_ln_b, L0_ffn_gate_w, L0_ffn_gate_b, L0_ffn_W1, L0_ffn_b1, L0_ffn_W2, L0_ffn_b2):

    def _L0_attn_a_ref(x, Wqkv, bqkv, Wproj, bproj):
        import jax, jax.numpy as jnp
        import numpy as np
        B, T, C = x.shape
        n_head = 16
        hd = C // n_head
        x_proj = x @ Wqkv + bqkv
        q = x_proj[:, :, :C].reshape(B, n_head, T, hd)
        k = x_proj[:, :, C:2 * C].reshape(B, n_head, T, hd)
        v = x_proj[:, :, 2 * C:].reshape(B, n_head, T, hd)
        att = jnp.einsum('bhtd,bhsd->bhts', q, k) * (1.0 / jnp.sqrt(jnp.float32(hd)))
        causal = jnp.tril(jnp.ones((T, T), dtype=bool))
        att = jnp.where(causal, att, jnp.float32(-jnp.inf))
        att = jax.nn.softmax(att, axis=-1)
        y = att @ v
        y = jnp.transpose(y, (0, 2, 1, 3)).reshape(B, T, C)
        return y @ Wproj + bproj

    def _L0_attn_b_ref(x, ln_w, ln_b, W_in, dt_bias, A_log, D, rms_w, W_out):
        import jax, jax.numpy as jnp
        import numpy as np
        DIM = 128
        D_STATE = 32
        HEADDIM = 64
        EXPAND = 2
        CHUNK = 64
        D_INNER = EXPAND * DIM
        NHEADS = D_INNER // HEADDIM
        ROPE_DIM = int(0.5 * D_STATE)
        D_IN_PROJ = 2 * D_INNER + 2 * D_STATE + NHEADS
        B_SZ = 4
        L = 512

        def _segsum(a):
            T = a.shape[-1]
            cs = jnp.cumsum(a, axis=-1)
            d = cs[..., :, None] - cs[..., None, :]
            mask = jnp.tril(jnp.ones((T, T), bool))
            return jnp.where(mask, d, -jnp.inf)

        def _rope(v):
            t = jnp.arange(v.shape[1], dtype=jnp.float32)
            inv_freq = 1.0 / 10000.0 ** (jnp.arange(0, ROPE_DIM, 2, dtype=jnp.float32) / ROPE_DIM)
            ang = t[:, None] * inv_freq[None, :]
            cos, sin = (jnp.cos(ang)[None], jnp.sin(ang)[None])
            vr, vp = (v[..., :ROPE_DIM], v[..., ROPE_DIM:])
            v1, v2 = (vr[..., 0::2], vr[..., 1::2])
            r = jnp.stack([v1 * cos - v2 * sin, v1 * sin + v2 * cos], axis=-1)
            return jnp.concatenate([r.reshape(vr.shape), vp], axis=-1)
        B, Ls, _ = x.shape
        mu = jnp.mean(x, -1, keepdims=True)
        var = jnp.var(x, -1, keepdims=True)
        h = (x - mu) * jax.lax.rsqrt(var + 1e-06) * ln_w + ln_b
        zxbcdt = h @ W_in
        z = zxbcdt[..., :D_INNER]
        xs = jax.nn.silu(zxbcdt[..., D_INNER:2 * D_INNER])
        Bc = jax.nn.silu(zxbcdt[..., 2 * D_INNER:2 * D_INNER + D_STATE])
        Cc = jax.nn.silu(zxbcdt[..., 2 * D_INNER + D_STATE:2 * D_INNER + 2 * D_STATE])
        dt = jax.nn.softplus(zxbcdt[..., -NHEADS:] + dt_bias)
        Bc, Cc = (_rope(Bc), _rope(Cc))
        A = -jnp.exp(A_log)
        xh = xs.reshape(B, Ls, NHEADS, HEADDIM)
        nc = Ls // CHUNK
        Xc = (xh * dt[..., None]).reshape(B, nc, CHUNK, NHEADS, HEADDIM)
        a = (dt * A).reshape(B, nc, CHUNK, NHEADS).transpose(0, 3, 1, 2)
        Bk = Bc.reshape(B, nc, CHUNK, D_STATE)
        Ck = Cc.reshape(B, nc, CHUNK, D_STATE)
        A_cs = jnp.cumsum(a, axis=-1)
        Lmat = jnp.exp(_segsum(a))
        scores = jnp.einsum('bcln,bcsn->bcls', Ck, Bk)
        M = scores[:, None] * Lmat
        Yd = jnp.einsum('bhcls,bcshp->bclhp', M, Xc)
        decay_states = jnp.exp(A_cs[..., -1:] - A_cs)
        states = jnp.einsum('bcln,bhcl,bclhp->bchpn', Bk, decay_states, Xc)
        states = jnp.concatenate([jnp.zeros_like(states[:, :1]), states], axis=1)
        dc = jnp.exp(_segsum(jnp.pad(A_cs[..., -1], ((0, 0), (0, 0), (1, 0)))))
        states_in = jnp.einsum('bhzc,bchpn->bzhpn', dc, states)[:, :-1]
        Yo = jnp.einsum('bcln,bchpn,bhcl->bclhp', Ck, states_in, jnp.exp(A_cs))
        y = (Yd + Yo).reshape(B, Ls, NHEADS, HEADDIM) + xh * D[None, None, :, None]
        y = y.reshape(B, Ls, D_INNER)
        y = y * jax.nn.silu(z)
        y = y * jax.lax.rsqrt(jnp.mean(y * y, -1, keepdims=True) + 1e-06) * rms_w
        return x + y @ W_out

    def _L0_ffn_ref(x, norm1_w, norm2_w, Wq, Wdkv, Wuk, Wuv, Wo, ln_g, ln_b, gate_w, gate_b, W1, b1, W2, b2):
        import jax, jax.numpy as jnp
        import numpy as np
        D_MODEL = 128
        N_HEADS = 16
        HEAD_DIM = D_MODEL // N_HEADS
        KV_LATENT = 64
        N_EXPERTS = 4
        D_HIDDEN = 4 * D_MODEL
        B, T = (2, 128)

        def rmsnorm(x, w, eps=1e-06):
            return w * (x * jax.lax.rsqrt(jnp.mean(x * x, axis=-1, keepdims=True) + eps))

        def layernorm(x, g, b, eps=1e-05):
            mu = jnp.mean(x, axis=-1, keepdims=True)
            var = jnp.mean((x - mu) ** 2, axis=-1, keepdims=True)
            return (x - mu) * jax.lax.rsqrt(var + eps) * g + b

        def apply_rope(x):
            t, d = (x.shape[2], x.shape[3])
            half = d // 2
            pos = jnp.arange(t, dtype=x.dtype)[:, None]
            inv_freq = 1.0 / 10000.0 ** (jnp.arange(half, dtype=x.dtype) / half)
            ang = pos * inv_freq[None, :]
            sin, cos = (jnp.sin(ang), jnp.cos(ang))
            x1, x2 = (x[..., :half], x[..., half:])
            return jnp.concatenate([x1 * cos - x2 * sin, x1 * sin + x2 * cos], axis=-1)

        def mla_attention(x, Wq, Wdkv, Wuk, Wuv, Wo, ln_g, ln_b):
            b, t, _ = x.shape
            q = (x @ Wq.T).reshape(b, t, N_HEADS, HEAD_DIM).transpose(0, 2, 1, 3)
            latent = layernorm(x @ Wdkv.T, ln_g, ln_b)
            k = (latent @ Wuk.T).reshape(b, t, N_HEADS, HEAD_DIM).transpose(0, 2, 1, 3)
            v = (latent @ Wuv.T).reshape(b, t, N_HEADS, HEAD_DIM).transpose(0, 2, 1, 3)
            q = apply_rope(q)
            k = apply_rope(k)
            scores = jnp.einsum('bhqd,bhkd->bhqk', q, k) / np.sqrt(HEAD_DIM)
            causal = jnp.tril(jnp.ones((t, t), dtype=bool))
            scores = jnp.where(causal, scores, -jnp.inf)
            attn = jax.nn.softmax(scores, axis=-1)
            out = jnp.einsum('bhqk,bhkd->bhqd', attn, v).transpose(0, 2, 1, 3).reshape(b, t, D_MODEL)
            return out @ Wo.T

        def moe(x, gate_w, gate_b, W1, b1, W2, b2):
            logits = x @ gate_w.T + gate_b
            top = jnp.argmax(logits, axis=-1)
            onehot = jax.nn.one_hot(top, N_EXPERTS, dtype=x.dtype)
            h = jax.nn.relu(jnp.einsum('btd,ehd->bteh', x, W1) + b1)
            y = jnp.einsum('bteh,edh->bted', h, W2) + b2
            return jnp.einsum('bted,bte->btd', y, onehot)
        x = x + mla_attention(rmsnorm(x, norm1_w), Wq, Wdkv, Wuk, Wuv, Wo, ln_g, ln_b)
        x = x + moe(rmsnorm(x, norm2_w), gate_w, gate_b, W1, b1, W2, b2)
        return x
    x = L0_attn_a_x
    x = x + _L0_attn_a_ref(_layernorm(x, axis=-1), L0_attn_a_Wqkv, L0_attn_a_bqkv, L0_attn_a_Wproj, L0_attn_a_bproj)
    x = x + _L0_ffn_ref(_layernorm(x, axis=-1), L0_ffn_norm1_w, L0_ffn_norm2_w, L0_ffn_Wq, L0_ffn_Wdkv, L0_ffn_Wuk, L0_ffn_Wuv, L0_ffn_Wo, L0_ffn_ln_g, L0_ffn_ln_b, L0_ffn_gate_w, L0_ffn_gate_b, L0_ffn_W1, L0_ffn_b1, L0_ffn_W2, L0_ffn_b2)
    x = x + _L0_attn_b_ref(_layernorm(x, axis=-1), L0_attn_b_ln_w, L0_attn_b_ln_b, L0_attn_b_W_in, L0_attn_b_dt_bias, L0_attn_b_A_log, L0_attn_b_D, L0_attn_b_rms_w, L0_attn_b_W_out)
    x = x + _L0_ffn_ref(_layernorm(x, axis=-1), L0_ffn_norm1_w, L0_ffn_norm2_w, L0_ffn_Wq, L0_ffn_Wdkv, L0_ffn_Wuk, L0_ffn_Wuv, L0_ffn_Wo, L0_ffn_ln_g, L0_ffn_ln_b, L0_ffn_gate_w, L0_ffn_gate_b, L0_ffn_W1, L0_ffn_b1, L0_ffn_W2, L0_ffn_b2)
    return x

_drawn_inputs = setup_inputs


def setup_inputs(seed=0):
    import zlib

    import numpy as np

    out = dict(_drawn_inputs(seed))
    spreads = {'L0_attn_b_ln_w': (1.0, 0.2),
     'L0_attn_b_ln_b': (0.0, 0.293),
     'L0_attn_b_rms_w': (1.0, 0.563),
     'L0_ffn_norm1_w': (1.0, 0.2),
     'L0_ffn_norm2_w': (1.0, 0.2),
     'L0_ffn_ln_g': (1.0, 0.2),
     'L0_ffn_ln_b': (0.0, 0.1),
     'L0_ffn_gate_b': (0.0, 0.1),
     'L0_ffn_b1': (0.0, 0.1),
     'L0_ffn_b2': (0.0, 0.1)}
    factors = {'L0_attn_b_dt_bias': 8.0, 'L0_attn_b_A_log': 8.0, 'L0_attn_b_D': 5.66}
    for name, (base, spread) in spreads.items():
        noise = np.random.default_rng([zlib.crc32(name.encode()), seed]).standard_normal(out[name].shape)
        drawn = base * np.exp(spread * noise) if base else spread * noise
        out[name] = jnp.asarray(drawn.astype(out[name].dtype))
    for name, factor in factors.items():
        out[name] = (out[name] * factor).astype(out[name].dtype)
    return out
```

```python
from contextlib import ExitStack

import numpy as np
import concourse.bass as bass
from concourse import mybir

F32 = mybir.dt.float32
BF16 = mybir.dt.bfloat16
ALU = mybir.AluOpType
ACT = mybir.ActivationFunctionType
AX = mybir.AxisListType

P = 128
NB, T, C = 16, 256, 128
NT = T // P
H, HD = 16, 8
G, CL = 4, 4
LAT = 64
NE, DH = 4, 512
HC = DH // P
DI, DS, MH, MP = 256, 32, 4, 64
KQ = 6 * HD
KM = KQ + 3
UNITS = 12
VPITCH = H * (P + HD)
SCALE = float(HD) ** -0.5
MASKED = -1e30


class Batch:

    def __init__(self, layer, x, residue, ring, count=NB):
        self.layer, self.x, self.ring, self.count = layer, x, ring, count
        self.m = residue % ring
        self.n = x + layer * count
        self.uses = len(range(self.m, count, ring))
        self.quot = None

    def first(self, d):
        return isinstance(self.x, int) and self.x < d


def batch(layer, it, c, ring, count=NB):
    b = Batch(layer, c if it is None else it * ring + c, c, ring, count)
    b.use = layer * b.uses + (c // ring if it is None else it + c // ring)
    b.it, b.c = it, c
    return b


def back(b, d):
    if b.first(d):
        return None
    return batch(b.layer, b.it, b.c - d, b.ring, b.count)


def done(b, d, per):
    if b.first(d):
        return b.layer * b.count * per or None
    return (b.n - d + 1) * per


def wait(eng, sem, value):
    if value is None or (isinstance(value, int) and value <= 0):
        return
    eng.wait_ge(sem, value)


def bf16_bits(v):
    return (np.ascontiguousarray(v, dtype=np.float32).view(np.uint32) >> 16).astype(np.uint16)


def constants():
    i = np.arange(P)
    allowed_m = i[None, :] <= i[:, None]
    g, r, c = np.meshgrid(np.arange(G), np.arange(8), np.arange(CL), indexing="ij")
    t = (r * 16 + g * CL + c).reshape(-1)
    allowed_a = t[None, :] <= t[:, None]
    masks = []
    for ok in (allowed_a, allowed_a.T, allowed_m, allowed_m.T):
        masks.append(np.tile(np.where(ok, 0.0, MASKED), (1, 4)))
    half = HD // 2
    inv = (1.0 / 10000.0 ** (np.arange(half, dtype=np.float32) / half)).astype(np.float32)
    ang = (np.arange(T, dtype=np.float32)[:, None] * inv[None, :]).astype(np.float32)
    d = np.arange(C) % HD
    cos = np.cos(ang.astype(np.float64))[:, d % half].T
    sin = np.sin(ang.astype(np.float64))[:, d % half].T * np.where(d < half, -1.0, 1.0)[:, None]
    rd = DS // 2
    inv_s = (1.0 / 10000.0 ** (np.arange(0, rd, 2, dtype=np.float32) / rd)).astype(np.float32)
    ang_s = (np.arange(T, dtype=np.float32)[:, None] * inv_s[None, :]).astype(np.float64)
    cos_s, sin_s = np.ones((DS, T)), np.zeros((DS, T))
    turn = np.zeros((DS, DS))
    for j in range(rd):
        cos_s[j] = np.cos(ang_s[:, j // 2])
        sin_s[j] = np.sin(ang_s[:, j // 2])
        turn[j, j ^ 1] = -1.0 if j % 2 == 0 else 1.0
    le = (i[:, None] <= i[None, :]).astype(np.float32)
    f = np.float32
    part = np.zeros((3, 2))
    part[1:, 0] = 1.0
    part[2:, 1] = 1.0
    return {
        "c_ident": np.eye(P, dtype=f), "c_identb": bf16_bits(np.eye(P)),
        "c_masks": bf16_bits(np.concatenate(masks, 1)),
        "c_rope": np.concatenate([cos, sin], 1).astype(f),
        "c_rope_s": np.concatenate([cos_s, cos_s, sin_s, sin_s], 1).astype(f),
        "c_turn": np.ascontiguousarray(turn.T).astype(f),
        "c_after": (i[:, None] > i[None, :]).astype(f),
        "c_upto": np.concatenate([le, np.ones((P, P)), le], 1).astype(f),
        "c_rank": np.tile(np.arange(NE, 0, -1), (P, NE)).astype(f),
        "c_part": part.astype(f),
    }


def layouts(a):
    ac = np.ascontiguousarray
    w = a["L0_attn_a_Wqkv"]
    bq = a["L0_attn_a_bqkv"]
    op, d, g, c = np.meshgrid(np.arange(3), np.arange(HD), np.arange(G), np.arange(CL), indexing="ij")
    col = (op * C + (g * CL + c) * HD + d)
    cols = np.moveaxis(col, 3, 0).reshape(CL, 3 * HD * G)
    swap = np.arange(C).reshape(H, 2, HD // 2)[:, ::-1].reshape(-1)
    f = "L0_ffn_"
    out = {
        "a_w": ac(np.moveaxis(w[:, cols], 0, 0).reshape(C, -1)),
        "a_b": ac(bq[cols].T),
        "a_wo": a["L0_attn_a_Wproj"],
        "bias_rows": ac(np.concatenate([a[f + "b2"].reshape(-1), a["L0_attn_a_bproj"]])[None]),
        "m_wq": ac(np.concatenate([a[f + "Wq"].T, a[f + "Wq"].T[:, swap]], 1)),
        "m_wdkv": ac(a[f + "Wdkv"].T),
        "m_wuk": ac(np.concatenate([a[f + "Wuk"].T, a[f + "Wuk"].T[:, swap]], 1)),
        "m_wuv": ac(a[f + "Wuv"].T),
        "m_wo": ac(a[f + "Wo"].T),
        "cols": ac(np.stack([a[f + "norm1_w"], a[f + "norm2_w"], a["L0_attn_b_ln_w"], a["L0_attn_b_ln_b"],
                             a["L0_attn_b_rms_w"][:P], a["L0_attn_b_rms_w"][P:]], 1)),
        "lat_cols": ac(np.stack([a[f + "ln_g"], a[f + "ln_b"]], 1)),
        "rows": ac(np.concatenate([a[f + "gate_b"]] * 4 + [a["L0_attn_b_dt_bias"]] * 2
                                  + [a["L0_attn_b_A_log"], a["L0_attn_b_D"]])[None]),
        "e_gate": ac(a[f + "gate_w"].T),
        "e_w1": ac(np.transpose(a[f + "W1"], (2, 0, 1)).reshape(C, NE * DH)),
        "e_b1": ac(a[f + "b1"].reshape(NE * HC, P).T),
        "e_w2": ac(np.transpose(a[f + "W2"].reshape(NE, C, HC, P), (3, 0, 2, 1)).reshape(P, -1)),
        "s_win": a["L0_attn_b_W_in"],
        "s_wout": ac(np.transpose(a["L0_attn_b_W_out"].reshape(2, P, C), (1, 0, 2)).reshape(P, -1)),
    }
    return {k: ac(v) for k, v in out.items()}


def program(nc, x_in, w, out, layers="AFSF"):
    with ExitStack() as ctx:
        def sb(name, shape, dt=F32):
            return ctx.enter_context(nc.sbuf_tensor(name, shape, dt))

        def sem(name):
            return ctx.enter_context(nc.semaphore(name))

        bank = [ctx.enter_context(nc.psum_tensor(f"bank{i}", [P, 512], F32)) for i in range(8)]

        X = sb("X", [P, NB * T])
        X1 = sb("X1", [P, NB * T])
        W = {}
        for k, v in w.items():
            if k == "bias_rows":
                W[k] = sb("w_" + k, [3, v.shape[1]])
            elif k == "rows":
                W[k] = sb("w_" + k, [P, v.shape[1]])
            else:
                W[k] = sb("w_" + k, list(v.shape), v.dtype)
        ident = W["c_ident"]
        identb, mask_tiles = W["c_identb"].bitcast(BF16), W["c_masks"].bitcast(BF16)
        NBIAS = NE * C + C
        bias_parts = sb("bias_parts", [3, NBIAS], BF16)
        b2_rows = sb("b2_rows", [3, NE * 4 * C], BF16)
        ones3 = sb("ones3", [3, P], BF16)
        ones = sb("ones", [P, P])
        power = sb("power", [P, 4])
        a_neg = sb("a_neg", [P, MH])

        st = sb("st", [P, 4, 6])
        mv = sb("mv", [P, 4, 2])
        rs = sb("rs", [P, 8, 4])
        XN = sb("XN", [P, 4 * P])
        HT = sb("HT", [P, 2, 512])
        lst = sb("lst", [P, 2, 6])
        lmv = sb("lmv", [P, 2, 2])
        lrs = sb("lrs", [P, 2, 2])
        LN = sb("LN", [P, 2, LAT])
        LT = sb("LT", [LAT, T])
        roped = sb("roped", [P, 2, 512])
        RT = sb("RT", [P, 3, T])
        QKVG = sb("QKVG", [3 * HD * G, H * 64])
        VT = sb("VT", [P, T])
        rest = sb("rest", [P, 2, T])
        parts = sb("parts", [P, 2, 3, T], BF16)
        q_tiles = [sb(f"q_tile{i}", [P, H * T], BF16) for i in range(2)]
        k_tiles = [sb(f"k_tile{i}", [P, H * T], BF16) for i in range(2)]

        def rows_of(tiles, m, lo, hi):
            base = 64 * (m % 2)
            return tiles[m // 2][base + lo:base + hi, :]
        VZ = [sb(f"VZ{i}", [P, NT * VPITCH]) for i in range(3)]
        NM = sb("NM", [P, H, 2])
        nm_rest = sb("nm_rest", [P, 2 * H])
        NMP = sb("NMP", [P, 3, 2 * H], BF16)
        NMT = sb("NMT", [6 * H, P], BF16)
        PR = sb("PR", [P, 4, 512])
        REC = sb("REC", [P, T])
        YT = sb("YT", [P, T])

        bias_r = HT[0:3, :, :].rearrange("p a t -> p (a t)")[:, 0:NBIAS]
        bias_hi = XN[0:3, 0:NBIAS // 2].bitcast(BF16)
        bias_mid = QKVG[0:3, 0:NBIAS // 2].bitcast(BF16)

        LG = sb("LG", [P, 16])
        gmax = sb("gmax", [P, 2, 4])
        geq = sb("geq", [P, 2, 16])
        OH = sb("OH", [P, 2, 16])
        HID = [q[:, :].bitcast(F32).rearrange("p (c t) -> p c t", c=HC) for q in q_tiles]
        YE = sb("YE", [P, 2, 512])

        part_dram = nc.dram_tensor("part_dram", (3, 2, 3, HD, H, T), BF16).ap()
        a_dram = nc.dram_tensor("a_dram", (3, H, 3 * HD * G, 64), F32).ap()

        names = """settled ones_rows loaded x_loaded const_set vz_zeroed bias_split
            scores_ready score_maxed max_split max_T max_rows
            st_ready exps_done pv_done y_recip y_normed y_projected resid_added
            x_bn x_moments rstd_steps x_normed xT_ready hT_ready
            lat_ready q_ready lat_bn lat_moments lat_rstd lat_normed latT_psum latT_ready k_ready v_ready
            rope_product roped_sum v_placed part_hi part_rest part_mid part_lo
            a_proj a_v_ordered a_evac_act a_evac_dve
            e_bn e_moments e_rstd e_normed e_xT e_hT e_logits e_route e_acc
            hid_ready hid_act hid_dve ye_ready ye_masked ye_added out_done""".split()
        S = {n: sem(n) for n in names}
        parts_written = [sem(f"parts_written{i}") for i in range(3)]
        qk_packed = [sem(f"qk_packed{i}") for i in range(3)]
        maxrow_landed = [sem(f"maxrow_landed{i}") for i in range(3)]
        a_written = [sem(f"a_written{i}") for i in range(3)]
        a_loaded = [sem(f"a_loaded{i}") for i in range(3)]

        N_LOADS = len(w)

        def xcols(b):
            return bass.ds(b.x * T, T)

        def xtile(b, t):
            return bass.ds(b.x * T + t * P, P)

        def tile_order(ap):
            return ap.rearrange("p (g x c) -> p x g c", g=G, x=NT)

        def settle(eng):
            eng.sem_inc(S["settled"], 1)

        def cnt(kind, b, a_per, m_per, k):
            if kind == "A":
                return b.x * a_per + k
            return NB * a_per + (b.n - NB) * m_per + k

        def dve_stats(dve, kind, b):
            wait(dve, S["rstd_steps"], cnt(kind, b, 2, 7, 0))
            wait(dve, S["x_normed"], cnt(kind, b, 2, 4, 0))
            for t in range(NT):
                dve.bn_stats(st[:, t, :], X[:, xtile(b, t)]).then_inc(S["x_bn"], 1)
            dve.wait_ge(S["x_bn"], b.n * 2 + 2)
            settle(dve)
            for t in range(NT):
                dve.bn_aggr(mv[:, t, :], st[:, t, :]).then_inc(S["x_moments"], 1)

        def dve_norm(dve, kind, b):
            dve.wait_ge(S["rstd_steps"], cnt(kind, b, 2, 7, 2 if kind == "A" else 7))
            wait(dve, S["xT_ready"], b.n)
            r = 1 if kind == "A" else 6
            for t in range(NT):
                dve.tensor_scalar(XN[:, t * P:(t + 1) * P], X[:, xtile(b, t)], mv[:, t, 0:1],
                                  rs[:, r, t:t + 1], ALU.subtract, ALU.mult).then_inc(S["x_normed"], 1)
            if kind == "M":
                for t in range(NT):
                    dve.tensor_scalar(X1[:, xtile(b, t)], X[:, xtile(b, t)], mv[:, t, 0:1],
                                      rs[:, 1, t:t + 1], ALU.subtract, ALU.mult).then_inc(S["x_normed"], 1)

        def dve_a_evac(dve, b):
            dve.wait_ge(S["a_proj"], b.x * 2 + 2)
            wait(dve, a_written[(b.m + 2) % 3], prev_use(b, 1, 16))
            for c in (2, 3):
                dve.tensor_scalar(QKVG[:, :].rearrange("p (t c) -> p c t", c=CL)[:, c, :],
                                  bank[6][0:96, (c - 2) * T:(c - 1) * T], W["a_b"][:, c:c + 1], None,
                                  ALU.add).then_inc(S["a_evac_dve"], 1)

        def dve_rope(dve, b, which):
            dve.wait_ge(S["q_ready" if which == 0 else "k_ready"], b.n - NB + 1)
            wait(dve, S["roped_sum"], (b.n - NB) * 2 + which)
            dve.tensor_tensor(roped[:, which, :], bank[7][:, :], W["c_rope"][:, :],
                              ALU.mult).then_inc(S["rope_product"], 1)
            dve.wait_ge(S["rope_product"], (b.n - NB) * 2 + which + 1)
            wait(dve, S["part_rest"], b.n * 2)
            wait(dve, S["part_hi"], b.n * 2)
            dve.tensor_tensor(RT[:, which, :], roped[:, which, 0:T], roped[:, which, T:2 * T],
                              ALU.add).then_inc(S["roped_sum"], 1)

        def dve_lat_stats(dve, b):
            n = b.n - NB
            dve.wait_ge(S["lat_ready"], n + 1)
            wait(dve, S["lat_rstd"], n * 2)
            wait(dve, S["lat_normed"], n * 2)
            for t in range(NT):
                dve.bn_stats(lst[:, t, :], bank[6][:, t * LAT:(t + 1) * LAT]).then_inc(S["lat_bn"], 1)
            dve.wait_ge(S["lat_bn"], n * 2 + 2)
            settle(dve)
            for t in range(NT):
                dve.bn_aggr(lmv[:, t, :], lst[:, t, :]).then_inc(S["lat_moments"], 1)

        def dve_lat_norm(dve, b):
            n = b.n - NB
            dve.wait_ge(S["lat_rstd"], n * 2 + 2)
            wait(dve, S["latT_psum"], n)
            for t in range(NT):
                dve.tensor_scalar(LN[:, t, :], bank[6][:, t * LAT:(t + 1) * LAT], lmv[:, t, 0:1],
                                  lrs[:, 1, t:t + 1], ALU.subtract, ALU.mult).then_inc(S["lat_normed"], 1)

        def split_source(kind, op):
            return tile_order(RT[:, op, :]) if kind == "A" else RT[:, op, :]

        def as_source(kind, ap):
            return ap.rearrange("p (x g c) -> p x g c", g=G, x=NT) if kind == "A" else ap

        def dve_split(dve, kind, b, op):
            dve.wait_ge(S["part_hi"], b.n * 2 + op + 1)
            wait(dve, S["part_lo"], b.n * 2)
            dve.tensor_tensor(as_source(kind, rest[:, op, :]), split_source(kind, op),
                              as_source(kind, parts[:, op, 0, :]), ALU.subtract).then_inc(S["part_rest"], 1)
            dve.wait_ge(S["part_rest"], b.n * 2 + op + 1)
            dve.tensor_copy(parts[:, op, 1, :], rest[:, op, :]).then_inc(S["part_mid"], 1)

        def dve_max(dve, b, u):
            dve.wait_ge(S["scores_ready"], b.n * UNITS + u + 1)
            if u == 0:
                wait(dve, S["max_split"], b.n * 4)
            q, j = u // 3, u % 3
            src = bank[3 + u % 2]
            if j < 2:
                h = 4 * q + 2 * j
                dve.tensor_reduce(NM[:, h:h + 2, 1], src[:, :].rearrange("p (h k) -> p h k", h=2),
                                  AX.X, ALU.max, negate=True).then_inc(S["score_maxed"], 1)
            else:
                dve.tensor_reduce(NM[:, 4 * q:4 * q + 4, 0], src[:, :].rearrange("p (h k) -> p h k", h=4),
                                  AX.X, ALU.max, negate=True).then_inc(S["score_maxed"], 1)

        def dve_y(dve, kind, b):
            dve.wait_ge(S["pv_done"], (b.n + 1) * UNITS)
            wait(dve, S["y_normed"], b.n * 4)
            for half in range(2):
                lo, other = slice(64 * half, 64 * half + 64), slice(64 - 64 * half, 128 - 64 * half)
                dve.reciprocal(REC[lo, :], bank[5][other, half * T:(half + 1) * T]).then_inc(S["y_recip"], 1)
            wait(dve, S["y_projected"], b.n)
            for half in range(2):
                lo = slice(64 * half, 64 * half + 64)
                dve.wait_ge(S["y_recip"], b.n * 2 + half + 1)
                for t in range(NT):
                    src = bank[5][lo, half * T + t * P:half * T + (t + 1) * P]
                    rec = REC[lo, t * P:(t + 1) * P]
                    dst = YT[lo, t * P:(t + 1) * P]
                    if kind == "A":
                        src = src.rearrange("p (g r c) -> p g r c", g=G, c=CL)
                        rec = rec.rearrange("p (g r c) -> p g r c", g=G, c=CL)
                        dst = dst.rearrange("p (r g c) -> p g r c", g=G, c=CL)
                    dve.tensor_tensor(dst, src, rec, ALU.mult).then_inc(S["y_normed"], 1)

        def dve_resid(dve, kind, b):
            dve.wait_ge(S["y_projected"], b.n + 1)
            dst = X if kind == "A" else X1
            dve.tensor_tensor(dst[:, xcols(b)], dst[:, xcols(b)], bank[6][:, 0:T],
                              ALU.add).then_inc(S["resid_added"], 1)

        def pool_rstd(pool, kind, b):
            pool.wait_ge(S["x_moments"], b.n * 2 + 2)
            s0 = cnt(kind, b, 2, 7, 0)
            wait(pool, S["x_normed"], cnt(kind, b, 2, 4, 0))
            rstd_chain(pool, S["rstd_steps"], s0, mv[:, 0:2, 1], rs, 2, kind != "A")

        def rstd_chain(pool, s, s0, var, rs, n, double):
            r = lambda k: rs[:, k, 0:n]
            settle(pool)
            pool.tensor_scalar(r(0), var, 1e-5, None, ALU.add).then_inc(s, 1)
            pool.wait_ge(s, s0 + 1)
            settle(pool)
            pool.tensor_tensor(r(1), r(0), power[:, 0:n], ALU.pow).then_inc(s, 1)
            if not double:
                return
            pool.wait_ge(s, s0 + 2)
            settle(pool)
            pool.tensor_tensor(r(2), r(1), r(1), ALU.mult).then_inc(s, 1)
            pool.wait_ge(s, s0 + 3)
            settle(pool)
            pool.tensor_tensor(r(3), r(2), var, ALU.mult).then_inc(s, 1)
            pool.wait_ge(s, s0 + 4)
            settle(pool)
            pool.tensor_scalar(r(4), r(3), 1e-6, None, ALU.add).then_inc(s, 1)
            pool.wait_ge(s, s0 + 5)
            settle(pool)
            pool.tensor_tensor(r(5), r(4), power[:, 0:n], ALU.pow).then_inc(s, 1)
            pool.wait_ge(s, s0 + 6)
            settle(pool)
            pool.tensor_tensor(r(6), r(5), r(1), ALU.mult).then_inc(s, 1)

        def pool_lat_rstd(pool, b):
            n = b.n - NB
            pool.wait_ge(S["lat_moments"], n * 2 + 2)
            wait(pool, S["lat_normed"], n * 2)
            settle(pool)
            pool.tensor_scalar(lrs[:, 0, :], lmv[:, :, 1], 1e-5, None, ALU.add).then_inc(S["lat_rstd"], 1)
            pool.wait_ge(S["lat_rstd"], n * 2 + 1)
            settle(pool)
            pool.tensor_tensor(lrs[:, 1, :], lrs[:, 0, :], power[:, 0:2], ALU.pow).then_inc(S["lat_rstd"], 1)

        def pool_split(pool, b, op):
            pool.wait_ge(S["part_mid"], b.n * 2 + op + 1)
            wait(pool, parts_written[(b.m + 2) % 3], prev_use(b, 1, 96))
            settle(pool)
            pool.tensor_tensor(parts[:, op, 2, :], rest[:, op, :], parts[:, op, 1, :],
                               ALU.subtract).then_inc(S["part_lo"], 1)

        def pool_a_v(pool, b):
            pool.wait_ge(a_loaded[b.m], b.use * 48 + 48)
            wait(pool, S["k_ready_a"], b.x)
            settle(pool)
            pool.tensor_copy(VT[:, :].rearrange("p (x g c) -> p x g c", g=G, x=NT),
                             tile_order(RT[:, 2, :])).then_inc(S["a_v_ordered"], 1)

        def pool_max_split(pool, b):
            nm = NM[:, :, :].rearrange("p h x -> p (h x)")
            pool.wait_ge(S["score_maxed"], (b.n + 1) * UNITS)
            wait(pool, S["max_T"], b.n)
            settle(pool)
            pool.tensor_copy(NMP[:, 0, :], nm).then_inc(S["max_split"], 1)
            pool.wait_ge(S["max_split"], b.n * 4 + 1)
            settle(pool)
            pool.tensor_tensor(nm_rest[:, :], nm, NMP[:, 0, :], ALU.subtract).then_inc(S["max_split"], 1)
            pool.wait_ge(S["max_split"], b.n * 4 + 2)
            settle(pool)
            pool.tensor_copy(NMP[:, 1, :], nm_rest[:, :]).then_inc(S["max_split"], 1)
            pool.wait_ge(S["max_split"], b.n * 4 + 3)
            settle(pool)
            pool.tensor_tensor(NMP[:, 2, :], nm_rest[:, :], NMP[:, 1, :], ALU.subtract).then_inc(S["max_split"], 1)

        def act_hT(act, kind, b):
            act.wait_ge(S["xT_ready"], b.n + 1)
            if kind == "A":
                wait(act, S["a_proj"], b.x * 2)
                act.activation(HT[:, 0, 0:T], bank[6][:, 0:T], ACT.Copy).then_inc(S["hT_ready"], 1)
            else:
                wait(act, S["q_ready"], b.n - NB)
                act.activation(HT[:, 0, 0:T], bank[6][:, 0:T], ACT.Identity,
                               scale=W["cols"][:, 0:1]).then_inc(S["hT_ready"], 1)

        def act_a_evac(act, b):
            act.wait_ge(S["a_proj"], b.x * 2 + 1)
            wait(act, a_written[(b.m + 2) % 3], prev_use(b, 1, 16))
            for c in (0, 1):
                act.activation(QKVG[:, :].rearrange("p (t c) -> p c t", c=CL)[:, c, :],
                               bank[7][0:96, c * T:(c + 1) * T], ACT.Identity,
                               bias=W["a_b"][:, c:c + 1]).then_inc(S["a_evac_act"], 1)

        def act_latT(act, b):
            n = b.n - NB
            act.wait_ge(S["latT_psum"], n + 1)
            wait(act, S["v_ready"], n)
            act.activation(LT[:, :], bank[6][0:LAT, 0:T], ACT.Identity, scale=W["lat_cols"][:, 0:1],
                           bias=W["lat_cols"][:, 1:2]).then_inc(S["latT_ready"], 1)

        def act_v(act, kind, b):
            act.wait_ge(S["v_ready"] if kind == "M" else S["k_ready_a"], (b.n - NB if kind == "M" else b.x) + 1)
            wait(act, S["pv_done"], done(b, 3, UNITS))
            src = bank[6] if kind == "M" else bank[7]
            for t in range(NT):
                dst = VZ[b.m][:, t * VPITCH:(t + 1) * VPITCH].rearrange("p (h c) -> p h c", h=H)[:, :, 0:HD]
                act.activation(dst, src[:, t * P:(t + 1) * P].rearrange("p (h d) -> p h d", h=H),
                               ACT.Copy).then_inc(S["v_placed"], 1)

        def act_split(act, kind, b, op):
            if kind == "A":
                act.wait_ge(a_loaded[b.m], b.use * 48 + 48)
            else:
                act.wait_ge(S["roped_sum"], (b.n - NB) * 2 + op + 1)
            wait(act, parts_written[(b.m + 2) % 3], prev_use(b, 1, 96))
            wait(act, S["part_rest"], b.n * 2)
            act.activation(as_source(kind, parts[:, op, 0, :]), split_source(kind, op),
                           ACT.Copy).then_inc(S["part_hi"], 1)

        def act_max_rows(act, b):
            act.wait_ge(S["max_T"], b.n + 1)
            wait(act, maxrow_landed[(b.m + 2) % 3], prev_use(b, 1, 16))
            act.activation(NMT[:, :], bank[3][0:6 * H, 0:P // 2].bitcast(BF16),
                           ACT.Copy).then_inc(S["max_rows"], 1)

        def act_exp(act, b, u):
            act.wait_ge(S["st_ready"], b.n * UNITS + u + 1)
            wait(act, S["pv_done"], b.n * UNITS + u - 3)
            act.activation(PR[:, u % 4, :], bank[u % 3][:, :], ACT.Exp,
                           scale=SCALE).then_inc(S["exps_done"], 1)

        def pe_T(pe, kind, b):
            pe.wait_ge(S["x_normed"], cnt(kind, b, 2, 4, 2))
            bank6_free(pe, kind, b)
            for t in range(NT):
                mm = pe.transpose(bank[6][:, t * P:(t + 1) * P], XN[:, t * P:(t + 1) * P], ident[:, :])
            mm.then_inc(S["xT_ready"], 1)

        def bank6_free(pe, kind, b):
            if kind == "A":
                wait(pe, S["a_evac_dve"], b.x * 2)
                if not b.first(3):
                    pe.wait_ge(S["resid_added"], b.n - 2)
            else:
                wait(pe, S["v_placed"], b.n * 2)
                wait(pe, S["resid_added"], done(b, 3, 1))

        def pe_a_proj(pe, b):
            pe.wait_ge(S["hT_ready"], b.n + 1)
            wait(pe, S["v_placed"], b.n * 2)
            for c in range(CL):
                mm = pe.matmul(bank[7 if c < 2 else 6][0:96, (c % 2) * T:(c % 2 + 1) * T],
                               W["a_w"][:, c * 96:(c + 1) * 96], HT[:, 0, 0:T], start=True, stop=True)
                if c % 2:
                    mm.then_inc(S["a_proj"], 1)

        def pe_a_v(pe, b):
            pe.wait_ge(S["a_v_ordered"], b.x + 1)
            pe.wait_ge(S["a_evac_act"], b.x * 2 + 2)
            for t in range(NT):
                mm = pe.transpose(bank[7][:, t * P:(t + 1) * P], VT[:, t * P:(t + 1) * P], ident[:, :])
            mm.then_inc(S["k_ready_a"], 1)

        def pe_qlat(pe, b):
            n = b.n - NB
            pe.wait_ge(S["hT_ready"], b.n + 1)
            for t in range(NT):
                mm = pe.matmul(bank[6][:, t * LAT:(t + 1) * LAT], HT[:, 0, t * P:(t + 1) * P],
                               W["m_wdkv"][:, :], start=True, stop=True)
            mm.then_inc(S["lat_ready"], 1)
            wait(pe, S["rope_product"], n * 2)
            for r in range(2):
                mm = pe.matmul(bank[7][:, r * T:(r + 1) * T], W["m_wq"][:, r * P:(r + 1) * P], HT[:, 0, 0:T],
                               start=True, stop=True)
            mm.then_inc(S["q_ready"], 1)

        def pe_latT(pe, b):
            n = b.n - NB
            pe.wait_ge(S["lat_normed"], n * 2 + 2)
            settle(pe)
            for t in range(NT):
                mm = pe.transpose(bank[6][0:LAT, t * P:(t + 1) * P], LN[:, t, :], ident[:, :])
            mm.then_inc(S["latT_psum"], 1)

        def pe_kv(pe, b):
            n = b.n - NB
            pe.wait_ge(S["latT_ready"], n + 1)
            pe.wait_ge(S["rope_product"], n * 2 + 1)
            for r in range(2):
                mm = pe.matmul(bank[7][:, r * T:(r + 1) * T], W["m_wuk"][:, r * P:(r + 1) * P], LT[:, :],
                               start=True, stop=True)
            mm.then_inc(S["k_ready"], 1)
            for t in range(NT):
                mm = pe.matmul(bank[6][:, t * P:(t + 1) * P], LT[:, t * P:(t + 1) * P], W["m_wuv"][:, :],
                               start=True, stop=True)
            mm.then_inc(S["v_ready"], 1)

        def score_unit(pe, b, u, keys_out, mask, rows, dst, ready):
            q, j = u // 3, u % 3
            qp = rows_of(q_tiles, b.m, 0, rows).rearrange("p (h t) -> p h t", h=H)
            kp = rows_of(k_tiles, b.m, 0, rows).rearrange("p (h t) -> p h t", h=H)
            lhs, rhs = (kp, qp) if keys_out else (qp, kp)
            full, alone = (0, 1) if keys_out else (1, 0)
            if j < 2:
                for i in range(2):
                    h = 4 * q + 2 * j + i
                    pe.matmul(dst[:, i * T:(i + 1) * T], lhs[:, h, full * P:(full + 1) * P], rhs[:, h, :],
                              start=(i == 0), stop=False, skip_group_check=True)
                pe.matmul(dst[:, :].rearrange("p (i t) -> p i t", i=2)[:, :, full * P:(full + 1) * P],
                          identb[:, :], mask[:, 0:2 * P], start=False, stop=True,
                          skip_group_check=True).then_inc(ready, 1)
            else:
                for i in range(4):
                    h = 4 * q + i
                    pe.matmul(dst[:, i * P:(i + 1) * P], lhs[:, h, alone * P:(alone + 1) * P],
                              rhs[:, h, alone * P:(alone + 1) * P], start=(i == 0), stop=False,
                              skip_group_check=True)
                pe.matmul(dst[:, :], identb[:, :], mask, start=False, stop=True,
                          skip_group_check=True).then_inc(ready, 1)

        def masks(kind, keys_out):
            i = (0 if kind == "A" else 2) + keys_out
            return mask_tiles[:, i * 512:(i + 1) * 512]

        def pe_s(pe, kind, b, u):
            if u == 0:
                pe.wait_ge(qk_packed[b.m], b.use * 96 + 96)
                wait(pe, S["max_rows"], b.n)
            wait(pe, S["score_maxed"], b.n * UNITS + u - 1)
            score_unit(pe, b, u, 0, masks(kind, 0), KQ, bank[3 + u % 2], S["scores_ready"])

        def pe_max_T(pe, b):
            pe.wait_ge(S["max_split"], b.n * 4 + 4)
            pe.transpose(bank[3][0:6 * H, 0:P // 2].bitcast(BF16),
                         NMP[:, :, :].rearrange("p a n -> p (a n)"), identb[:, :]).then_inc(S["max_T"], 1)

        def pe_st(pe, kind, b, u):
            if u == 0:
                pe.wait_ge(maxrow_landed[b.m], b.use * 16 + 16)
            wait(pe, S["exps_done"], b.n * UNITS + u - 2)
            score_unit(pe, b, u, 1, masks(kind, 1), KM, bank[u % 3], S["st_ready"])

        def pe_pv(pe, b, u):
            if u == 0:
                pe.wait_ge(S["v_placed"], b.n * 2 + 2)
                wait(pe, S["y_normed"], b.n * 4)
            pe.wait_ge(S["exps_done"], b.n * UNITS + u + 1)
            q, j = u // 3, u % 3
            half = q // 2
            vz = lambda t, h: VZ[b.m][:, t * VPITCH + h * P:t * VPITCH + (h + 1) * P]
            if j < 2:
                for i in range(2):
                    mm = pe.matmul(bank[5][:, half * T:(half + 1) * T], vz(0, 4 * q + 2 * j + i),
                                   PR[:, u % 4, i * T:(i + 1) * T], start=(u % 6 == 0 and i == 0), stop=False,
                                   skip_group_check=True)
            else:
                for i in range(4):
                    mm = pe.matmul(bank[5][:, half * T + P:(half + 1) * T], vz(1, 4 * q + i),
                                   PR[:, u % 4, i * P:(i + 1) * P], start=False, stop=(u % 6 == 5),
                                   skip_group_check=True)
            mm.then_inc(S["pv_done"], 1)

        def pe_project(pe, kind, b):
            pe.wait_ge(S["y_normed"], b.n * 4 + 4)
            if kind == "A":
                pe.wait_ge(S["a_evac_dve"], min2(b.x + 3, NB) * 2)
            else:
                pe.wait_ge(S["v_placed"], (b.layer * NB + min2(b.x + 3, NB)) * 2)
            for t in range(NT):
                if kind == "A":
                    pe.matmul(bank[6][:, t * P:(t + 1) * P], ones3[:, :], bias_parts[:, NE * C:], start=(t == 0),
                              stop=False, skip_group_check=True)
                mm = pe.matmul(bank[6][:, t * P:(t + 1) * P], YT[:, t * P:(t + 1) * P],
                               W["a_wo" if kind == "A" else "m_wo"][:, :], start=(kind != "A" and t == 0),
                               stop=True, skip_group_check=True)
            mm.then_inc(S["y_projected"], 1)

        def min2(a, b):
            return min(a, b) if isinstance(a, int) else a

        def prev_use(b, d, per):
            p = back(b, d)
            if p is None:
                return None
            return p.use * per + per

        def sp_a(sp, b):
            sp.wait_ge(S["a_evac_act"], b.x * 2 + 2)
            sp.wait_ge(S["a_evac_dve"], b.x * 2 + 2)
            sp.dma_start(a_dram[b.m].rearrange("h r t -> r h t"),
                         QKVG[:, :].rearrange("r (h t) -> r h t", h=H)).then_inc(a_written[b.m], 16)
            sp.wait_ge(a_written[b.m], b.use * 16 + 16)
            wait(sp, S["part_rest"], b.n * 2)
            wait(sp, S["k_ready_a"], b.x)
            src = a_dram[b.m].rearrange("h (o d g) t -> o h d (g t)", o=3, g=G)
            for op in range(3):
                sp.dma_start(RT[:, op, :], src[op]).then_inc(a_loaded[b.m], 16)

        def sp_pack(sp, b):
            sp.wait_ge(S["part_lo"], b.n * 2 + 2)
            for op in range(2):
                for i in range(3):
                    sp.dma_start(part_dram[b.m, op, i].rearrange("d h t -> h d t"),
                                 parts[:, op, i, :]).then_inc(parts_written[b.m], 16)
            sp.wait_ge(parts_written[b.m], b.use * 96 + 96)
            settle(sp)
            wait(sp, S["st_ready"], done(b, 3, UNITS))
            settle(sp)
            flat = part_dram[b.m].rearrange("o i d h t -> o i d (h t)")
            row = 0
            for i in range(3):
                n = 3 - i
                sp.dma_start(rows_of(q_tiles, b.m, row, row + n * HD),
                             flat[0, i:i + 1].broadcast_to([n, HD, H * T])).then_inc(qk_packed[b.m], 16)
                sp.dma_start(rows_of(k_tiles, b.m, row, row + n * HD), flat[1, 0:n]).then_inc(qk_packed[b.m], 16)
                row += n * HD

        def sp_max(sp, b):
            sp.wait_ge(S["max_rows"], b.n + 1)
            sp.dma_start(rows_of(q_tiles, b.m, KQ, KM).rearrange("p (n t) -> p n t", t=P),
                         NMT[:, :]).then_inc(maxrow_landed[b.m], 16)

        def attention_slot(kind, pre, mx, ex, fin):
            order = []
            prelude = {0: ["stats"], 1: ["norm"], 2: ["T"], 3: ["proj"], 5: ["latnorm", "latT"], 7: ["kv"],
                       9: ["split0"], 10: ["split1", "pack"]}
            if kind == "A":
                prelude = {0: ["stats"], 1: ["norm"], 2: ["T"], 3: ["proj"], 10: ["kv", "split0", "split1", "pack"]}
            for u in range(UNITS):
                if ex is not None:
                    order.append(("st", ex, u))
                if u == 1 and fin is not None:
                    order.append(("project", fin, 0))
                if pre is not None:
                    order += [(s, pre, 0) for s in prelude.get(u, [])]
                if mx is not None and 3 <= u < 9:
                    order += [("s", mx, 2 * (u - 3)), ("s", mx, 2 * (u - 3) + 1)]
                if mx is not None and u == 9:
                    order.append(("max", mx, 0))
                if ex is not None and u >= 2:
                    order.append(("pv", ex, u - 2))
            if ex is not None:
                order += [("pv", ex, UNITS - 2), ("pv", ex, UNITS - 1), ("y", ex, 0)]
            return order

        def attention(eng, part, kind, layer):
            def slot(it, c):
                at = lambda d: None if it is None and not 0 <= c - d < NB else batch(layer, it, c - d, 3)
                for step, b, u in attention_slot(kind, at(0), at(1), at(2), at(3)):
                    part(eng, kind, step, b, u)
            for c in range(3):
                slot(None, c)
            with eng.Fori(0, (NB - 4) // 3) as it:
                for c in range(3, 6):
                    slot(it, c)
            for c in range(NB - 1, NB + 3):
                slot(None, c)

        def dve_part(dve, kind, step, b, u):
            if step == "stats":
                dve_stats(dve, kind, b)
            elif step == "norm":
                dve_norm(dve, kind, b)
            elif step == "proj" and kind == "A":
                dve_a_evac(dve, b)
            elif step == "proj":
                dve_lat_stats(dve, b)
                dve_rope(dve, b, 0)
            elif step == "latnorm" and kind == "M":
                dve_lat_norm(dve, b)
            elif step == "kv" and kind == "M":
                dve_rope(dve, b, 1)
            elif step in ("split0", "split1"):
                dve_split(dve, kind, b, int(step[-1]))
            elif step == "s":
                dve_max(dve, b, u)
            elif step == "y":
                dve_y(dve, kind, b)
            elif step == "project":
                dve_resid(dve, kind, b)

        def pool_part(pool, kind, step, b, u):
            if step == "stats":
                pool_rstd(pool, kind, b)
            elif step == "proj" and kind == "M":
                pool_lat_rstd(pool, b)
            elif step == "kv" and kind == "A":
                pool_a_v(pool, b)
            elif step in ("split0", "split1"):
                pool_split(pool, b, int(step[-1]))
            elif step == "max":
                pool_max_split(pool, b)

        def act_part(act, kind, step, b, u):
            if step == "T":
                act_hT(act, kind, b)
            elif step == "proj" and kind == "A":
                act_a_evac(act, b)
            elif step == "latT" and kind == "M":
                act_latT(act, b)
            elif step == "kv":
                act_v(act, kind, b)
            elif step in ("split0", "split1"):
                act_split(act, kind, b, int(step[-1]))
            elif step == "max":
                act_max_rows(act, b)
            elif step == "st":
                act_exp(act, b, u)

        def pe_part(pe, kind, step, b, u):
            if step == "T":
                pe_T(pe, kind, b)
            elif step == "proj":
                pe_a_proj(pe, b) if kind == "A" else pe_qlat(pe, b)
            elif step == "latT" and kind == "M":
                pe_latT(pe, b)
            elif step == "kv":
                pe_a_v(pe, b) if kind == "A" else pe_kv(pe, b)
            elif step == "s":
                pe_s(pe, kind, b, u)
            elif step == "max":
                pe_max_T(pe, b)
            elif step == "st":
                pe_st(pe, kind, b, u)
            elif step == "pv":
                pe_pv(pe, b, u)
            elif step == "project":
                pe_project(pe, kind, b)

        def sp_part(sp, kind, step, b, u):
            if step == "proj" and kind == "A":
                sp_a(sp, b)
            elif step == "pack":
                sp_pack(sp, b)
            elif step == "max":
                sp_max(sp, b)

        S["k_ready_a"] = sem("a_v_ready")

        NU = NB // 2
        HID_BANK = (0, 1, 2, 5)

        def e_cols(b, t=None):
            return bass.ds(b.x * 2 * T, 2 * T) if t is None else bass.ds(b.x * 2 * T + t * P, P)

        def dve_e_stats(dve, b):
            wait(dve, S["e_rstd"], b.n * 4)
            for t in range(4):
                dve.bn_stats(st[:, t, :], X1[:, e_cols(b, t)]).then_inc(S["e_bn"], 1)
            dve.wait_ge(S["e_bn"], b.n * 4 + 4)
            settle(dve)
            for t in range(4):
                dve.bn_aggr(mv[:, t, :], st[:, t, :]).then_inc(S["e_moments"], 1)

        def pool_e_rstd(pool, b):
            s, v = S["e_rstd"], b.n * 4
            pool.wait_ge(S["e_moments"], v + 4)
            wait(pool, S["e_normed"], v)
            settle(pool)
            pool.tensor_tensor(rs[:, 0, :], mv[:, :, 0], mv[:, :, 0], ALU.mult).then_inc(s, 1)
            pool.wait_ge(s, v + 1)
            settle(pool)
            pool.tensor_tensor(rs[:, 1, :], rs[:, 0, :], mv[:, :, 1], ALU.add).then_inc(s, 1)
            pool.wait_ge(s, v + 2)
            settle(pool)
            pool.tensor_scalar(rs[:, 2, :], rs[:, 1, :], 1e-6, None, ALU.add).then_inc(s, 1)
            pool.wait_ge(s, v + 3)
            settle(pool)
            pool.tensor_tensor(rs[:, 3, :], rs[:, 2, :], power[:, :], ALU.pow).then_inc(s, 1)
            pool.tensor_tensor(X[:, e_cols(b)], X[:, e_cols(b)], X1[:, e_cols(b)], ALU.add).then_inc(S["e_acc"], 1)

        def dve_e_norm(dve, b):
            dve.wait_ge(S["e_rstd"], b.n * 4 + 4)
            wait(dve, S["e_xT"], b.n)
            for t in range(4):
                dve.tensor_scalar(XN[:, t * P:(t + 1) * P], X1[:, e_cols(b, t)], rs[:, 3, t:t + 1], None,
                                  ALU.mult).then_inc(S["e_normed"], 1)

        def pe_e_T(pe, b):
            pe.wait_ge(S["e_normed"], b.n * 4 + 4)
            wait(pe, S["e_hT"], b.n)
            for t in range(4):
                mm = pe.transpose(bank[6][:, t * P:(t + 1) * P], XN[:, t * P:(t + 1) * P], ident[:, :])
            mm.then_inc(S["e_xT"], 1)

        def act_e_hT(act, b):
            act.wait_ge(S["e_xT"], b.n + 1)
            wait(act, S["hid_ready"], done(b, 2, NE * HC))
            act.activation(HT[:, b.m, :], bank[6][:, :], ACT.Identity,
                           scale=W["cols"][:, 1:2]).then_inc(S["e_hT"], 1)

        def pe_e_gate(pe, b):
            pe.wait_ge(S["e_hT"], b.n + 1)
            wait(pe, S["e_route"], b.n * 6)
            for t in range(4):
                mm = pe.matmul(bank[7][:, t * NE:(t + 1) * NE], HT[:, b.m, t * P:(t + 1) * P], W["e_gate"][:, :],
                               start=True, stop=True)
            mm.then_inc(S["e_logits"], 1)

        def dve_e_route(dve, b):
            s, v = S["e_route"], b.n * 6
            grp = lambda ap: ap.rearrange("p (t e) -> p t e", e=NE)
            wide = lambda ap: ap.unsqueeze(2).broadcast_to([P, 4, NE])
            dve.wait_ge(S["e_logits"], b.n + 1)
            wait(dve, S["ye_masked"], done(b, 2, NE))
            dve.tensor_tensor(LG[:, :], bank[7][:, 0:16], W["rows"][:, 0:16], ALU.add).then_inc(s, 1)
            dve.wait_ge(s, v + 1)
            dve.tensor_reduce(gmax[:, 0, :], grp(LG[:, :]), AX.X, ALU.max).then_inc(s, 1)
            dve.wait_ge(s, v + 2)
            dve.tensor_tensor(grp(geq[:, 0, :]), grp(LG[:, :]), wide(gmax[:, 0, :]), ALU.is_equal).then_inc(s, 1)
            dve.wait_ge(s, v + 3)
            dve.tensor_tensor(geq[:, 1, :], geq[:, 0, :], W["c_rank"][:, :], ALU.mult).then_inc(s, 1)
            dve.wait_ge(s, v + 4)
            dve.tensor_reduce(gmax[:, 1, :], grp(geq[:, 1, :]), AX.X, ALU.max).then_inc(s, 1)
            dve.wait_ge(s, v + 5)
            dve.tensor_tensor(grp(OH[:, b.m, :]), grp(geq[:, 1, :]), wide(gmax[:, 1, :]), ALU.is_equal).then_inc(s, 1)

        def pe_e_hid(pe, b, e):
            if e == 0:
                pe.wait_ge(S["e_hT"], b.n + 1)
            for i in range(HC):
                c = e * HC + i
                wait(pe, S["hid_act" if c % 2 == 0 else "hid_dve"], b.n * (NE * HC // 2) + (c - 4) // 2 + 1)
                pe.matmul(bank[HID_BANK[c % 4]][:, :], W["e_w1"][:, c * P:(c + 1) * P], HT[:, b.m, :],
                          start=True, stop=True).then_inc(S["hid_ready"], 1)

        def e_evac(eng, b, e, odd):
            for i in range(odd, HC, 2):
                c = e * HC + i
                eng.wait_ge(S["hid_ready"], b.n * NE * HC + c + 1)
                wait(eng, S["ye_ready"], b.n * NE + e - 1)
                src, dst, bias = bank[HID_BANK[c % 4]][:, :], HID[e % 2][:, i, :], W["e_b1"][:, c:c + 1]
                if odd:
                    eng.tensor_scalar(dst, src, bias, 0.0, ALU.add, ALU.max).then_inc(S["hid_dve"], 1)
                else:
                    eng.activation(dst, src, ACT.Relu, bias=bias).then_inc(S["hid_act"], 1)

        def pe_e_y(pe, b, e):
            v = b.n * 8 + 2 * e + 2
            pe.wait_ge(S["hid_act"], v)
            pe.wait_ge(S["hid_dve"], v)
            wait(pe, S["ye_masked"], b.n * NE + e - 1)
            dst = bank[3 + e % 2]
            pe.matmul(dst[:, :], ones3[:, :], b2_rows[:, e * 4 * C:(e + 1) * 4 * C], start=True, stop=False,
                      skip_group_check=True)
            for t in range(4):
                for i in range(HC):
                    c = e * HC + i
                    mm = pe.matmul(dst[:, t * P:(t + 1) * P], HID[e % 2][:, i, t * P:(t + 1) * P],
                                   W["e_w2"][:, c * P:(c + 1) * P], start=False, stop=(i == HC - 1),
                                   skip_group_check=True)
            mm.then_inc(S["ye_ready"], 1)

        def dve_e_mask(dve, b, e):
            dve.wait_ge(S["ye_ready"], b.n * NE + e + 1)
            if e == 0:
                dve.wait_ge(S["e_route"], b.n * 6 + 6)
            wait(dve, S["ye_added"], b.n * NE + e - 1)
            oh = OH[:, b.m, :].rearrange("p (t e) -> p t e", e=NE)[:, :, e:e + 1].broadcast_to([P, 4, P])
            dve.tensor_tensor(YE[:, e % 2, :].rearrange("p (t c) -> p t c", t=4),
                              bank[3 + e % 2][:, :].rearrange("p (t c) -> p t c", t=4), oh,
                              ALU.mult).then_inc(S["ye_masked"], 1)

        def pool_e_add(pool, b, e):
            pool.wait_ge(S["ye_masked"], b.n * NE + e + 1)
            if e == 0:
                pool.wait_ge(S["e_acc"], b.n + 1)
            else:
                pool.wait_ge(S["ye_added"], b.n * NE + e)
            settle(pool)
            pool.tensor_tensor(X[:, e_cols(b)], X[:, e_cols(b)], YE[:, e % 2, :], ALU.add).then_inc(S["ye_added"], 1)

        def sp_out(sp, b):
            sp.wait_ge(S["ye_added"], (b.n + 1) * NE)
            sp.dma_start(out[bass.ds(b.x * 2 * T, 2 * T), :].rearrange("(t p) c -> p t c", p=P),
                         X[:, e_cols(b)].rearrange("p (t c) -> p t c", c=C)).then_inc(S["out_done"], 16)

        def expert_slot(part, eng, pre, b):
            def do(step, x, e=0):
                if x is not None:
                    part(eng, step, x, e)
            do("stats", pre)
            do("hid", b, 0)
            do("norm", pre)
            do("hid", b, 1)
            do("T", pre)
            do("y", b, 0)
            do("gate", pre)
            do("hid", b, 2)
            do("y", b, 1)
            do("hid", b, 3)
            do("y", b, 2)
            do("y", b, 3)
            do("out", b)

        def experts(eng, part, layer):
            def slot(it, c):
                at = lambda d: None if it is None and not 0 <= c - d < NU else batch(layer, it, c - d, 2, NU)
                expert_slot(part, eng, at(0), at(1))
            slot(None, 0)
            slot(None, 1)
            with eng.Fori(0, NU // 2 - 1) as it:
                slot(it, 2)
                slot(it, 3)
            slot(None, NU)

        last_e = layers.count("F") - 1

        def dve_e_part(dve, step, b, e):
            if step == "stats":
                dve_e_stats(dve, b)
            elif step == "norm":
                dve_e_norm(dve, b)
            elif step == "gate":
                dve_e_route(dve, b)
            elif step == "hid":
                e_evac(dve, b, e, 1)
            elif step == "y":
                dve_e_mask(dve, b, e)

        def act_e_part(act, step, b, e):
            if step == "T":
                act_e_hT(act, b)
            elif step == "hid":
                e_evac(act, b, e, 0)

        def pool_e_part(pool, step, b, e):
            if step == "stats":
                pool_e_rstd(pool, b)
            elif step == "y":
                pool_e_add(pool, b, e)

        def pe_e_part(pe, step, b, e):
            if step == "T":
                pe_e_T(pe, b)
            elif step == "gate":
                pe_e_gate(pe, b)
            elif step == "hid":
                pe_e_hid(pe, b, e)
            elif step == "y":
                pe_e_y(pe, b, e)

        def sp_e_part(sp, step, b, e):
            if step == "out" and b.layer == last_e and layers[-1] == "F":
                sp_out(sp, b)

        AD = sb("AD", [P, 2, NT * MH])
        dts = sb("dts", [P, 10, NT * MH])
        YN = sb("YN", [P, NT, DI])
        f32 = lambda t: t[:, :].bitcast(F32)
        SZ = f32(k_tiles[0]).rearrange("p (m t c) -> p m t c", m=2, t=NT)
        XD = f32(k_tiles[1])[:, 0:2 * NT * DI].rearrange("p (m t c) -> p m t c", m=2, t=NT)
        GM = f32(k_tiles[1])[:, 2 * NT * DI:2 * NT * DI + 6 * P].rearrange("p (m c) -> p m c", m=2)
        R0, R1 = f32(q_tiles[0])[:, 0:MH * T], f32(q_tiles[0])[:, MH * T:MH * (T + P)]
        L0, L1 = f32(q_tiles[1])[:, 0:MH * T], f32(q_tiles[1])[:, MH * T:MH * (T + P)]
        PRF = PR[:, :, :].rearrange("p a t -> p (a t)")
        M0, M1 = PRF[:, 0:MH * T], PRF[:, MH * T:MH * (T + P)]
        EZ = roped
        EB = rest[0:DS, :, :].rearrange("p a t -> p (a t)")
        BCS, BSIN = YE[0:DS, 0, :], YE[0:DS, 1, :]
        BCR, BCOS = QKVG[0:DS, 0:2 * T], QKVG[0:DS, 2 * T:4 * T]
        Y3 = RT[:, 0:2, :]
        YNT = parts[:, :, :, :].rearrange("p a b t -> p (a b t)").bitcast(F32)[:, 0:2 * T]
        DT, DT_STEPS = 9, 18
        for n in """s_bn s_moments s_rstd s_normed s_xT s_hT s_zx s_bc s_dt_ready s_eb s_ez s_dt s_u
                    s_bcs s_rot s_bcr s_bcos s_g s_gm s_silu s_xd s_r s_seg s_l s_m s_y s_ysum s_ybn s_ymoments
                    s_yr s_yn s_yT s_yTe s_out s_resid_added""".split():
            S[n] = sem(n)

        def dve_s_stats(dve, b):
            wait(dve, S["s_normed"], b.n * 5)
            for t in range(NT):
                dve.bn_stats(st[:, t, :], X[:, xtile(b, t)]).then_inc(S["s_bn"], 1)
            dve.wait_ge(S["s_bn"], b.n * 2 + 2)
            settle(dve)
            for t in range(NT):
                dve.bn_aggr(mv[:, t, :], st[:, t, :]).then_inc(S["s_moments"], 1)

        def pool_s_rstd(pool, b):
            pool.wait_ge(S["s_moments"], b.n * 2 + 2)
            rstd_chain(pool, S["s_rstd"], b.n * 7, mv[:, 0:2, 1], rs, 2, True)

        def dve_s_norm(dve, b):
            dve.wait_ge(S["s_rstd"], b.n * 7 + 7)
            wait(dve, S["s_xT"], b.n)
            for r, o in ((6, 0), (1, NT)):
                for t in range(NT):
                    dve.tensor_scalar(XN[:, (o + t) * P:(o + t + 1) * P], X[:, xtile(b, t)], mv[:, t, 0:1],
                                      rs[:, r, t:t + 1], ALU.subtract, ALU.mult).then_inc(S["s_normed"], 1)
            dve.wait_ge(S["s_normed"], b.n * 5 + 4)
            dve.tensor_tensor(X[:, xcols(b)], X[:, xcols(b)], XN[:, NT * P:2 * NT * P],
                              ALU.add).then_inc(S["s_normed"], 1)

        def pe_s_T(pe, b):
            pe.wait_ge(S["s_normed"], b.n * 5 + 2)
            wait(pe, S["s_hT"], b.n)
            wait(pe, S["s_dt"], b.n * DT_STEPS)
            for t in range(NT):
                mm = pe.transpose(bank[6][:, t * P:(t + 1) * P], XN[:, t * P:(t + 1) * P], ident[:, :])
            mm.then_inc(S["s_xT"], 1)

        def act_s_hT(act, b):
            act.wait_ge(S["s_xT"], b.n + 1)
            wait(act, S["s_dt_ready"], b.n)
            act.activation(HT[:, 0, 0:T], bank[6][:, 0:T], ACT.Identity, scale=W["cols"][:, 2:3],
                           bias=W["cols"][:, 3:4]).then_inc(S["s_hT"], 1)

        def pe_s_proj(pe, b):
            pe.wait_ge(S["s_hT"], b.n + 1)
            for t in range(NT):
                mm = pe.matmul(bank[6][:, T + t * MH:T + (t + 1) * MH], HT[:, 0, t * P:(t + 1) * P],
                               W["s_win"][:, 2 * DI + 2 * DS:], start=True, stop=True)
            mm.then_inc(S["s_dt_ready"], 1)
            wait(pe, S["s_bcs"], b.n * 3)
            for i in range(2):
                mm = pe.matmul(bank[2][0:DS, i * T:(i + 1) * T],
                               W["s_win"][:, 2 * DI + i * DS:2 * DI + (i + 1) * DS], HT[:, 0, 0:T],
                               start=True, stop=True)
            mm.then_inc(S["s_bc"], 1)
            wait(pe, S["s_silu"], b.n * 6)
            for t in range(NT):
                pe.matmul(bank[t][:, :], HT[:, 0, t * P:(t + 1) * P], W["s_win"][:, 0:2 * DI],
                          start=True, stop=True).then_inc(S["s_zx"], 1)

        def act_s_exps(act, b):
            act.wait_ge(S["s_bc"], b.n + 1)
            wait(act, S["s_bcs"], b.n * 3)
            act.activation(EB, bank[2][0:DS, :], ACT.Exp, scale=-1.0).then_inc(S["s_eb"], 1)
            wait(act, S["s_silu"], b.n * 6)
            for t in range(NT):
                act.wait_ge(S["s_zx"], b.n * 2 + t + 1)
                act.activation(EZ[:, t, :], bank[t][:, :], ACT.Exp, scale=-1.0).then_inc(S["s_ez"], 1)

        def dve_s_bc(dve, b):
            s, v = S["s_bcs"], b.n * 3
            dve.wait_ge(S["s_eb"], b.n + 1)
            wait(dve, S["s_bcr"], b.n * 2)
            dve.tensor_scalar(EB, EB, 1.0, None, ALU.add).then_inc(s, 1)
            dve.wait_ge(s, v + 1)
            dve.reciprocal(EB, EB).then_inc(s, 1)
            dve.wait_ge(s, v + 2)
            dve.tensor_tensor(BCS, bank[2][0:DS, :], EB, ALU.mult).then_inc(s, 1)

        def pe_s_rot(pe, b):
            pe.wait_ge(S["s_bcs"], b.n * 3 + 3)
            wait(pe, S["s_gm"], b.n)
            settle(pe)
            pe.matmul(bank[7][0:DS, :], W["c_turn"][:, :], BCS, start=True, stop=True).then_inc(S["s_rot"], 1)

        def pool_s_cos(pool, b):
            pool.wait_ge(S["s_bcs"], b.n * 3 + 3)
            wait(pool, S["s_bcr"], b.n * 2)
            settle(pool)
            pool.tensor_tensor(BCOS, BCS, W["c_rope_s"][:, 0:2 * T], ALU.mult).then_inc(S["s_bcos"], 1)

        def dve_s_rope(dve, b):
            dve.wait_ge(S["s_rot"], b.n + 1)
            dve.tensor_tensor(BSIN, bank[7][0:DS, :], W["c_rope_s"][:, 2 * T:], ALU.mult).then_inc(S["s_bcr"], 1)
            dve.wait_ge(S["s_bcos"], b.n + 1)
            dve.wait_ge(S["s_bcr"], b.n * 2 + 1)
            wait(dve, S["s_g"], b.n)
            dve.tensor_tensor(BCR, BSIN, BCOS, ALU.add).then_inc(S["s_bcr"], 1)

        def pe_s_g(pe, b):
            pe.wait_ge(S["s_bcr"], b.n * 2 + 2)
            pe.matmul(bank[7][:, 0:T], BCR[:, 0:P], BCR[:, T:2 * T], start=True, stop=True)
            pe.matmul(bank[7][:, T:T + P], BCR[:, P:T], BCR[:, T + P:2 * T], start=True,
                      stop=True).then_inc(S["s_g"], 1)

        def dve_s_gm(dve, b):
            dve.wait_ge(S["s_g"], b.n + 1)
            wait(dve, S["s_m"], done(b, 2, 2))
            dve.tensor_tensor(GM[:, b.m, :], bank[7][:, 0:3 * P], W["c_upto"][:, :], ALU.mult).then_inc(S["s_gm"], 1)

        def dve_s_dt(dve, b, second):
            s, v = S["s_dt"], b.n * DT_STEPS
            x, neg, mag, u, den, ratio, sq, poly, pos, dt = (dts[:, k, :] for k in range(10))

            def step(k, ins):
                ins.then_inc(s, 1)
                dve.wait_ge(s, v + k)
            if not second:
                dve.wait_ge(S["s_dt_ready"], b.n + 1)
                wait(dve, S["s_xd"], b.n * 4)
                step(1, dve.tensor_tensor(x, bank[6][:, T:T + NT * MH], W["rows"][:, 16:24], ALU.add))
                step(2, dve.tensor_scalar(neg, x, -1.0, None, ALU.mult))
                step(3, dve.tensor_tensor(mag, x, neg, ALU.max))
                return
            dve.wait_ge(S["s_u"], b.n + 1)
            step(4, dve.tensor_scalar(den, u, 2.0, None, ALU.add))
            step(5, dve.reciprocal(den, den))
            step(6, dve.tensor_tensor(ratio, u, den, ALU.mult))
            step(7, dve.tensor_tensor(sq, ratio, ratio, ALU.mult))
            step(8, dve.tensor_scalar(poly, sq, 1.0 / 15, None, ALU.mult))
            for k in range(6):
                step(9 + k, dve.scalar_tensor_tensor(poly, poly, 1.0 / (13 - 2 * k), sq, ALU.add, ALU.mult))
            step(15, dve.scalar_tensor_tensor(poly, poly, 1.0, ratio, ALU.add, ALU.mult))
            step(16, dve.tensor_scalar(pos, x, 0.0, None, ALU.max))
            step(17, dve.scalar_tensor_tensor(dt, poly, 2.0, pos, ALU.mult, ALU.add))
            wait(dve, S["s_r"], done(b, 2, 2))
            step(18, dve.tensor_tensor(AD[:, b.m, :].rearrange("p (t h) -> p t h", t=NT),
                                       dt.rearrange("p (t h) -> p t h", t=NT),
                                       a_neg[:, :].unsqueeze(1).broadcast_to([P, NT, MH]), ALU.mult))

        def act_s_dt(act, b):
            act.wait_ge(S["s_dt"], b.n * DT_STEPS + 3)
            act.activation(dts[:, 3, :], dts[:, 2, :], ACT.Exp, scale=-1.0).then_inc(S["s_u"], 1)

        def dve_s_silu(dve, b, t):
            s, v = S["s_silu"], b.n * 6 + 3 * t
            dve.wait_ge(S["s_ez"], b.n * 2 + t + 1)
            if t == 0:
                wait(dve, S["s_ysum"], done(b, 2, 4))
            dve.tensor_scalar(EZ[:, t, :], EZ[:, t, :], 1.0, None, ALU.add).then_inc(s, 1)
            dve.wait_ge(s, v + 1)
            dve.reciprocal(EZ[:, t, :], EZ[:, t, :]).then_inc(s, 1)
            dve.wait_ge(s, v + 2)
            dve.tensor_tensor(SZ[:, b.m, t, :], bank[t][:, :], EZ[:, t, :], ALU.mult).then_inc(s, 1)

        def pool_s_xd(pool, b):
            pool.wait_ge(S["s_silu"], b.n * 6 + 6)
            pool.wait_ge(S["s_dt"], b.n * DT_STEPS + 17)
            wait(pool, S["s_y"], done(b, 2, 1))
            heads = lambda ap: ap.rearrange("p (h c) -> p h c", h=MH)
            for t in range(NT):
                dt = dts[:, DT, t * MH:(t + 1) * MH].unsqueeze(2).broadcast_to([P, MH, MP])
                settle(pool)
                pool.tensor_tensor(heads(XD[:, b.m, t, :]), heads(SZ[:, b.m, t, DI:]), dt,
                                   ALU.mult).then_inc(S["s_xd"], 1)
            pool.wait_ge(S["s_xd"], b.n * 4 + 2)
            for t in range(NT):
                dd = W["rows"][:, 28:32].unsqueeze(2).broadcast_to([P, MH, MP])
                settle(pool)
                pool.tensor_tensor(heads(SZ[:, b.m, t, DI:]), heads(SZ[:, b.m, t, DI:]), dd,
                                   ALU.mult).then_inc(S["s_xd"], 1)

        def pool_s_r(pool, b):
            pool.wait_ge(S["s_dt"], b.n * DT_STEPS + 18)
            wait(pool, S["s_seg"], b.n * 3)
            for dst, t, cols, n in ((R0, 0, slice(0, T), T), (R1, 1, slice(T, T + P), P)):
                settle(pool)
                pool.tensor_tensor(dst.rearrange("p (h t) -> p h t", h=MH),
                                   W["c_upto"][:, cols].unsqueeze(1).broadcast_to([P, MH, n]),
                                   AD[:, b.m, t * MH:(t + 1) * MH].unsqueeze(2).broadcast_to([P, MH, n]),
                                   ALU.mult).then_inc(S["s_r"], 1)

        def pe_s_seg(pe, b):
            pe.wait_ge(S["s_r"], b.n * 2 + 2)
            wait(pe, S["s_ysum"], b.n * 4)
            for i in range(2):
                bk = bank[3 + i]
                pe.matmul(bk[:, :], W["c_after"][:, :], R0[:, i * 2 * T:(i + 1) * 2 * T], start=True, stop=False,
                          skip_group_check=True)
                pe.matmul(bk[:, :].rearrange("p (h t) -> p h t", h=2)[:, :, P:T], ones[:, :],
                          R1[:, i * 2 * P:(i + 1) * 2 * P], start=False, stop=True,
                          skip_group_check=True).then_inc(S["s_seg"], 1)
            wait(pe, S["s_resid_added"], b.n)
            pe.matmul(bank[5][:, :], W["c_after"][:, :], R1, start=True, stop=True).then_inc(S["s_seg"], 1)

        def act_s_l(act, b):
            wait(act, S["s_m"], b.n * 2)
            for i, dst in enumerate((L0[:, 0:2 * T], L0[:, 2 * T:4 * T], L1)):
                act.wait_ge(S["s_seg"], b.n * 3 + i + 1)
                act.activation(dst, bank[3 + i][:, :], ACT.Exp).then_inc(S["s_l"], 1)

        def dve_s_m(dve, b):
            dve.wait_ge(S["s_l"], b.n * 3 + 3)
            dve.wait_ge(S["s_gm"], b.n + 1)
            wait(dve, S["s_y"], b.n)
            for dst, src, cols, n in ((M0, L0, slice(0, T), T), (M1, L1, slice(T, T + P), P)):
                heads = lambda ap: ap.rearrange("p (h t) -> p h t", h=MH)
                dve.tensor_tensor(heads(dst), heads(src), GM[:, b.m, cols].unsqueeze(1).broadcast_to([P, MH, n]),
                                  ALU.mult).then_inc(S["s_m"], 1)

        def pe_s_y(pe, b):
            pe.wait_ge(S["s_m"], b.n * 2 + 2)
            pe.wait_ge(S["s_xd"], b.n * 4 + 2)
            for h in range(MH):
                pe.matmul(bank[3][:, h * MP:(h + 1) * MP], M0[:, h * T:h * T + P], XD[:, b.m, 0, h * MP:(h + 1) * MP],
                          start=(h == 0), stop=True, skip_group_check=True)
            for h in range(MH):
                dst = bank[4][:, h * MP:(h + 1) * MP]
                pe.matmul(dst, M0[:, h * T + P:(h + 1) * T], XD[:, b.m, 0, h * MP:(h + 1) * MP],
                          start=(h == 0), stop=False, skip_group_check=True)
                mm = pe.matmul(dst, M1[:, h * P:(h + 1) * P], XD[:, b.m, 1, h * MP:(h + 1) * MP],
                               start=False, stop=True, skip_group_check=True)
            mm.then_inc(S["s_y"], 1)

        def dve_s_gate(dve, b):
            dve.wait_ge(S["s_y"], b.n + 1)
            dve.wait_ge(S["s_xd"], b.n * 4 + 4)
            wait(dve, S["s_yn"], b.n * 2)
            for t in range(NT):
                dve.tensor_tensor(Y3[:, t, :], bank[3 + t][:, 0:DI], SZ[:, b.m, t, DI:], ALU.add).then_inc(S["s_ysum"], 1)
            dve.wait_ge(S["s_ysum"], b.n * 4 + 2)
            for t in range(NT):
                dve.tensor_tensor(Y3[:, t, :], Y3[:, t, :], SZ[:, b.m, t, 0:DI], ALU.mult).then_inc(S["s_ysum"], 1)
            dve.wait_ge(S["s_ysum"], b.n * 4 + 4)
            for t in range(NT):
                dve.bn_stats(lst[:, t, :], Y3[:, t, :]).then_inc(S["s_ybn"], 1)
            dve.wait_ge(S["s_ybn"], b.n * 2 + 2)
            wait(dve, S["s_yr"], b.n * 4)
            settle(dve)
            for t in range(NT):
                dve.bn_aggr(lmv[:, t, :], lst[:, t, :]).then_inc(S["s_ymoments"], 1)

        def pool_s_yr(pool, b):
            s, v = S["s_yr"], b.n * 4
            pool.wait_ge(S["s_ymoments"], b.n * 2 + 2)
            wait(pool, S["s_yn"], b.n * 2)
            settle(pool)
            pool.tensor_tensor(yrs[:, 0, :], lmv[:, :, 0], lmv[:, :, 0], ALU.mult).then_inc(s, 1)
            pool.wait_ge(s, v + 1)
            settle(pool)
            pool.tensor_tensor(yrs[:, 1, :], yrs[:, 0, :], lmv[:, :, 1], ALU.add).then_inc(s, 1)
            pool.wait_ge(s, v + 2)
            settle(pool)
            pool.tensor_scalar(yrs[:, 2, :], yrs[:, 1, :], 1e-6, None, ALU.add).then_inc(s, 1)
            pool.wait_ge(s, v + 3)
            settle(pool)
            pool.tensor_tensor(yrs[:, 3, :], yrs[:, 2, :], power[:, 0:2], ALU.pow).then_inc(s, 1)

        def dve_s_yn(dve, b):
            dve.wait_ge(S["s_yr"], b.n * 4 + 4)
            wait(dve, S["s_yT"], b.n)
            for t in range(NT):
                dve.tensor_scalar(YN[:, t, :], Y3[:, t, :], yrs[:, 3, t:t + 1], None, ALU.mult).then_inc(S["s_yn"], 1)

        def pe_s_yT(pe, b):
            pe.wait_ge(S["s_yn"], b.n * 2 + 2)
            for half in range(2):
                for t in range(NT):
                    mm = pe.transpose(bank[5][:, half * T + t * P:half * T + (t + 1) * P],
                                      YN[:, t, half * P:(half + 1) * P], ident[:, :])
            mm.then_inc(S["s_yT"], 1)

        def act_s_yT(act, b):
            act.wait_ge(S["s_yT"], b.n + 1)
            wait(act, S["s_out"], b.n)
            for half in range(2):
                act.activation(YNT[:, half * T:(half + 1) * T], bank[5][:, half * T:(half + 1) * T], ACT.Identity,
                               scale=W["cols"][:, 4 + half:5 + half]).then_inc(S["s_yTe"], 1)

        def pe_s_out(pe, b):
            pe.wait_ge(S["s_yTe"], b.n * 2 + 2)
            for t in range(NT):
                for half in range(2):
                    mm = pe.matmul(bank[5][:, t * P:(t + 1) * P], YNT[:, half * T + t * P:half * T + (t + 1) * P],
                                   W["s_wout"][:, half * P:(half + 1) * P], start=(t == 0 and half == 0),
                                   stop=(half == 1), skip_group_check=True)
            mm.then_inc(S["s_out"], 1)

        def dve_s_resid(dve, b):
            dve.wait_ge(S["s_out"], b.n + 1)
            dve.tensor_tensor(X[:, xcols(b)], X[:, xcols(b)], bank[5][:, 0:T], ALU.add).then_inc(S["s_resid_added"], 1)

        yrs = sb("yrs", [P, 4, 2])

        MIXER_ORDER = (("pre", "stats"), ("main", "seg"), ("pre", "norm"), ("pre", "proj"), ("pre", "exps"),
                       ("pre", "dt"), ("main", "mul"), ("pre", "dt2"), ("main", "gate"), ("pre", "bc"),
                       ("main", "yn"), ("pre", "rope"), ("main", "out"), ("pre", "gm"), ("pre", "silu"),
                       ("main", "resid"))

        def mixer(eng, part):
            def slot(it, c):
                at = lambda d: None if it is None and not 0 <= c - d < NB else batch(0, it, c - d, 2)
                for stage, step in MIXER_ORDER:
                    b = at(0 if stage == "pre" else 1)
                    if b is not None:
                        part(eng, step, b)
            slot(None, 0)
            slot(None, 1)
            with eng.Fori(0, NB // 2 - 1) as it:
                slot(it, 2)
                slot(it, 3)
            slot(None, NB)

        def dve_s_part(dve, step, b):
            if step == "stats":
                dve_s_stats(dve, b)
            elif step == "norm":
                dve_s_norm(dve, b)
            elif step == "dt":
                dve_s_dt(dve, b, False)
            elif step == "dt2":
                dve_s_dt(dve, b, True)
            elif step == "mul":
                dve_s_m(dve, b)
            elif step == "gate":
                dve_s_gate(dve, b)
            elif step == "bc":
                dve_s_bc(dve, b)
            elif step == "yn":
                dve_s_yn(dve, b)
            elif step == "rope":
                dve_s_rope(dve, b)
            elif step == "gm":
                dve_s_gm(dve, b)
            elif step == "silu":
                dve_s_silu(dve, b, 0)
                dve_s_silu(dve, b, 1)
            elif step == "resid":
                dve_s_resid(dve, b)

        def pool_s_part(pool, step, b):
            if step == "stats":
                pool_s_rstd(pool, b)
            elif step == "seg":
                pool_s_r(pool, b)
            elif step == "gate":
                pool_s_yr(pool, b)
            elif step == "rope":
                pool_s_cos(pool, b)
            elif step == "silu":
                pool_s_xd(pool, b)

        def act_s_part(act, step, b):
            if step == "norm":
                act_s_hT(act, b)
            elif step == "seg":
                act_s_l(act, b)
            elif step == "exps":
                act_s_exps(act, b)
            elif step == "dt":
                act_s_dt(act, b)
            elif step == "out":
                act_s_yT(act, b)

        def pe_s_part(pe, step, b):
            if step == "norm":
                pe_s_T(pe, b)
            elif step == "proj":
                pe_s_proj(pe, b)
            elif step == "seg":
                pe_s_seg(pe, b)
            elif step == "mul":
                pe_s_y(pe, b)
            elif step == "rope":
                pe_s_rot(pe, b)
            elif step == "gm":
                pe_s_g(pe, b)
            elif step == "out":
                pe_s_yT(pe, b)
                pe_s_out(pe, b)

        def sp_s_part(sp, step, b):
            pass

        def before(eng, i):
            if i == 0:
                eng.wait_ge(S["loaded"], 16 * N_LOADS)
                eng.wait_ge(S["x_loaded"], 16)
                eng.wait_ge(S["const_set"], 4)
                eng.wait_ge(S["ones_rows"], 3)
                eng.wait_ge(S["vz_zeroed"], 9)
                eng.wait_ge(S["bias_split"], 9)
                return
            kind = layers[i - 1]
            if kind == "S":
                eng.wait_ge(S["s_resid_added"], NB)
                if eng is nc.gpsimd:
                    ones_rows(eng, 3)
                if i < len(layers):
                    eng.wait_ge(S["ones_rows"], 6)
            elif kind == "F":
                eng.wait_ge(S["ye_added"], layers[:i].count("F") * NU * NE)
            else:
                eng.wait_ge(S["resid_added"], NB)

        def ones_rows(eng, n):
            for i in range(3):
                eng.memset(rows_of(k_tiles, i, 32, 64), 1.0).then_inc(S["ones_rows"], 1)
                eng.wait_ge(S["ones_rows"], n + i + 1)

        def run(eng, att, exp, mix):
            f = 0
            for i, kind in enumerate(layers):
                before(eng, i)
                if kind == "A":
                    attention(eng, att, "A", 0)
                elif kind == "F":
                    attention(eng, att, "M", f + 1)
                    eng.wait_ge(S["resid_added"], (f + 2) * NB)
                    experts(eng, exp, f)
                    f += 1
                else:
                    mixer(eng, mix)

        block = ctx.enter_context(nc.Block())

        @block.sync
        def _(sp):
            sp.dma_start(X[:, :].rearrange("p (t c) -> p t c", c=C),
                         x_in.rearrange("b (t p) c -> p (b t) c", p=P)).then_inc(S["x_loaded"], 16)
            for k, v in w.items():
                if k == "bias_rows":
                    sp.dma_start(W[k][:, :], v.broadcast_to([3, v.shape[1]])).then_inc(S["loaded"], 16)
                elif k == "rows":
                    sp.dma_start(W[k][:, :], v.broadcast_to([P, v.shape[1]])).then_inc(S["loaded"], 16)
                else:
                    sp.dma_start(W[k][:, :], v).then_inc(S["loaded"], 16)
            run(sp, sp_part, sp_e_part, sp_s_part)
            if layers[-1] == "F":
                sp.wait_ge(S["out_done"], 16 * NU)
            else:
                before(sp, len(layers))
                sp.dma_start(out.rearrange("(t p) c -> p t c", p=P),
                             X[:, :].rearrange("p (t c) -> p t c", c=C)).then_inc(S["out_done"], 16)
                sp.wait_ge(S["out_done"], 16)

        @block.gpsimd
        def _(pool):
            for i in range(3):
                pool.memset(VZ[i][:, :], 0.0).then_inc(S["vz_zeroed"], 1)
            pool.memset(ones3[:, :], 1.0).then_inc(S["const_set"], 1)
            pool.memset(ones[:, :], 1.0).then_inc(S["const_set"], 1)
            pool.memset(power[:, :], -0.5).then_inc(S["const_set"], 1)
            pool.wait_ge(S["vz_zeroed"], 3)
            for i in range(3):
                v = VZ[i][:, :].rearrange("p (t h c) -> p t h c", t=NT, h=H)
                pool.memset(v[:, :, 0:8, 64:72], 1.0).then_inc(S["vz_zeroed"], 1)
                pool.memset(v[:, :, 7:15, 72:80], 1.0).then_inc(S["vz_zeroed"], 1)
            pool.wait_ge(S["vz_zeroed"], 9)
            ones_rows(pool, 0)
            run(pool, pool_part, pool_e_part, pool_s_part)

        @block.vector
        def _(dve):
            s = S["bias_split"]
            dve.wait_ge(S["loaded"], 16 * N_LOADS)
            dve.tensor_copy(bias_hi, W["bias_rows"][:, :]).then_inc(s, 1)
            dve.wait_ge(s, 1)
            dve.tensor_scalar(bias_r, bias_hi, W["c_part"][:, 0:1], None, ALU.mult).then_inc(s, 1)
            dve.wait_ge(s, 2)
            dve.tensor_tensor(bias_r, W["bias_rows"][:, :], bias_r, ALU.subtract).then_inc(s, 1)
            dve.wait_ge(s, 3)
            dve.tensor_copy(bias_mid, bias_r).then_inc(s, 1)
            dve.wait_ge(s, 4)
            dve.tensor_scalar(bias_parts[:, :], bias_mid, W["c_part"][:, 1:2], None, ALU.mult).then_inc(s, 1)
            dve.wait_ge(s, 5)
            dve.tensor_tensor(bias_parts[:, :], bias_r, bias_parts[:, :], ALU.subtract).then_inc(s, 1)
            dve.wait_ge(s, 6)
            dve.tensor_copy(b2_rows[:, :].rearrange("p (e t c) -> p e t c", e=NE, t=4),
                            bias_parts[:, 0:NE * C].rearrange("p (e c) -> p e c", e=NE).unsqueeze(2)
                            .broadcast_to([3, NE, 4, C])).then_inc(s, 1)
            dve.wait_ge(s, 8)
            dve.tensor_scalar(a_neg[:, :], a_neg[:, :], -1.0, None, ALU.mult).then_inc(s, 1)
            dve.memset(gmax[:, :, :], 0.0).then_inc(S["const_set"], 1)
            run(dve, dve_part, dve_e_part, dve_s_part)

        @block.scalar
        def _(act):
            act.wait_ge(S["loaded"], 16 * N_LOADS)
            act.wait_ge(S["bias_split"], 7)
            act.activation(a_neg[:, :], W["rows"][:, 24:28], ACT.Exp).then_inc(S["bias_split"], 1)
            run(act, act_part, act_e_part, act_s_part)

        @block.tensor
        def _(pe):
            run(pe, pe_part, pe_e_part, pe_s_part)


LAYERS = "AFSF"
INPUTS = ["L0_attn_a_x"]


def kernel(**inputs):
    import concourse.bacc as bacc
    from concourse.bass_utils import run_bass_kernel_spmd as launch

    a = {k: np.asarray(v) for k, v in inputs.items()}
    nc = bacc.Bacc("TRN2", target_bir_lowering=False, num_devices=1)
    arrays = {"x": np.ascontiguousarray(a["L0_attn_a_x"])}
    arrays.update(layouts(a))
    arrays.update(constants())
    aps = {k: nc.dram_tensor(k, v.shape, mybir.dt.from_np(v.dtype), kind="ExternalInput").ap()
           for k, v in arrays.items()}
    out = nc.dram_tensor("out", (NB * T, C), F32, kind="ExternalOutput").ap()
    x_ap = aps.pop("x")
    program(nc, x_ap, aps, out, LAYERS)
    r = launch(nc, [arrays], core_ids=[0])
    return np.asarray(r.results[0]["out"]).reshape(NB, T, C)
```

```python
from contextlib import ExitStack

import numpy as np
import concourse.bass as bass
from concourse import mybir

F32 = mybir.dt.float32
BF16 = mybir.dt.bfloat16
F16 = mybir.dt.float16
ALU = mybir.AluOpType
ACT = mybir.ActivationFunctionType
AX = mybir.AxisListType

P = 128
NB, T, C = 16, 256, 128
NT = T // P
H, HD = 16, 8
G, CL = 4, 4
LAT = 64
NE, DH = 4, 512
HC = DH // P
DI, DS, MH, MP = 256, 32, 4, 64
KQ = 9 * HD
KM = KQ + 3
UNITS = 12
VW, VPITCH = 3 * HD + 1, 3 * HD + 2
EXP_SHIFT = 8 * float(np.log(2.0))
SCALE = float(HD) ** -0.5
MASKED = -1e30


class Batch:

    def __init__(self, layer, it, c, ring, count):
        n = layer * count + c
        loop = lambda v, step: v if it is None else it * step + v
        self.layer, self.ring, self.m = layer, ring, n % ring
        self.x, self.n, self.use = loop(c, ring), loop(n, ring), loop(n // ring, 1)
        self.use_before = loop((n - 1) // ring, 1)


def batch(layer, it, c, ring, count=NB):
    return Batch(layer, it, c, ring, count)


def done(b, d, per):
    return (b.n - d + 1) * per


def wait(eng, sem, value):
    if value is None or (isinstance(value, int) and value <= 0):
        return
    eng.wait_ge(sem, value)


def bf16_bits(v):
    return (np.ascontiguousarray(v, dtype=np.float32).view(np.uint32) >> 16).astype(np.uint16)


def constants():
    i = np.arange(P)
    allowed_m = i[None, :] <= i[:, None]
    g, r, c = np.meshgrid(np.arange(G), np.arange(8), np.arange(CL), indexing="ij")
    t = (r * 16 + g * CL + c).reshape(-1)
    allowed_a = t[None, :] <= t[:, None]
    masks = []
    for ok in (allowed_a, allowed_a.T, allowed_m, allowed_m.T):
        alone = np.where(ok, 0.0, MASKED)
        seen = np.zeros((P, P))
        queries_first = len(masks) % 2 == 0
        pair = np.concatenate([seen, alone] if queries_first else [alone, seen], 1)
        masks.append(np.concatenate([np.tile(pair, (1, 2)), np.tile(alone, (1, 4))], 1))
    half = HD // 2
    inv = (1.0 / 10000.0 ** (np.arange(half, dtype=np.float32) / half)).astype(np.float32)
    ang = (np.arange(T, dtype=np.float32)[:, None] * inv[None, :]).astype(np.float32)
    d = np.arange(C) % HD
    cos = np.cos(ang.astype(np.float64))[:, d % half].T
    sin = np.sin(ang.astype(np.float64))[:, d % half].T * np.where(d < half, -1.0, 1.0)[:, None]
    rd = DS // 2
    inv_s = (1.0 / 10000.0 ** (np.arange(0, rd, 2, dtype=np.float32) / rd)).astype(np.float32)
    ang_s = (np.arange(T, dtype=np.float32)[:, None] * inv_s[None, :]).astype(np.float64)
    cos_s, sin_s = np.ones((DS, T)), np.zeros((DS, T))
    turn = np.zeros((DS, DS))
    for j in range(rd):
        cos_s[j] = np.cos(ang_s[:, j // 2])
        sin_s[j] = np.sin(ang_s[:, j // 2])
        turn[j, j ^ 1] = -1.0 if j % 2 == 0 else 1.0
    le = (i[:, None] <= i[None, :]).astype(np.float32)
    f = np.float32
    part = np.zeros((3, 2))
    part[1:, 0] = 1.0
    part[2:, 1] = 1.0
    return {
        "c_ident": np.eye(P, dtype=f), "c_identb": bf16_bits(np.eye(P)),
        "c_masks": bf16_bits(np.concatenate(masks, 1)),
        "c_rope": np.concatenate([cos, sin], 1).astype(f),
        "c_rope_s": np.concatenate([cos_s, cos_s, sin_s, sin_s], 1).astype(f),
        "c_turn": np.ascontiguousarray(turn.T).astype(f),
        "c_after": (i[:, None] > i[None, :]).astype(f),
        "c_upto": np.concatenate([le, np.ones((P, P)), le], 1).astype(f),
        "c_upto16": (np.concatenate([le, np.ones((P, P)), le], 1) / 16).astype(f),
        "c_rank": np.tile(np.arange(NE, 0, -1), (P, NE)).astype(f),
        "c_part": part.astype(f),
    }


def layouts(a):
    ac = np.ascontiguousarray
    w = a["L0_attn_a_Wqkv"]
    bq = a["L0_attn_a_bqkv"]
    op, d, g, c = np.meshgrid(np.arange(3), np.arange(HD), np.arange(G), np.arange(CL), indexing="ij")
    col = (op * C + (g * CL + c) * HD + d)
    cols = np.moveaxis(col, 3, 0).reshape(CL, 3 * HD * G)
    swap = np.arange(C).reshape(H, 2, HD // 2)[:, ::-1].reshape(-1)
    f = "L0_ffn_"
    out = {
        "a_w": ac(np.moveaxis(w[:, cols], 0, 0).reshape(C, -1)),
        "a_b": ac(bq[cols].T),
        "a_wo": a["L0_attn_a_Wproj"],
        "bias_rows": ac(np.concatenate([a[f + "b2"].reshape(-1), a["L0_attn_a_bproj"]])[None]),
        "m_wq": ac(np.concatenate([a[f + "Wq"].T, a[f + "Wq"].T[:, swap]], 1)),
        "m_wdkv": ac(a[f + "Wdkv"].T),
        "m_wuk": ac(np.concatenate([a[f + "Wuk"].T, a[f + "Wuk"].T[:, swap]], 1)),
        "m_wuv": ac(a[f + "Wuv"].T),
        "m_wo": ac(a[f + "Wo"].T),
        "cols": ac(np.stack([a[f + "norm1_w"], a[f + "norm2_w"], a["L0_attn_b_ln_w"], a["L0_attn_b_ln_b"],
                             a["L0_attn_b_rms_w"][:P], a["L0_attn_b_rms_w"][P:]], 1)),
        "lat_cols": ac(np.stack([a[f + "ln_g"], a[f + "ln_b"]], 1)),
        "rows": ac(np.concatenate([a[f + "gate_b"]] * 4 + [a["L0_attn_b_dt_bias"]] * 2
                                  + [a["L0_attn_b_A_log"], a["L0_attn_b_D"]])[None]),
        "e_gate": ac(a[f + "gate_w"].T),
        "e_w1": ac(np.transpose(a[f + "W1"], (2, 0, 1)).reshape(C, NE * DH)),
        "e_b1": ac(a[f + "b1"].reshape(NE * HC, P).T),
        "e_w2": ac(np.transpose(a[f + "W2"].reshape(NE, C, HC, P), (3, 0, 2, 1)).reshape(P, -1)),
        "s_win": a["L0_attn_b_W_in"],
        "s_wout": ac(np.transpose(a["L0_attn_b_W_out"].reshape(2, P, C), (1, 0, 2)).reshape(P, -1)),
    }
    return {k: ac(v) for k, v in out.items()}


def program(nc, x_in, w, out, layers="AFSF"):
    with ExitStack() as ctx:
        def sb(name, shape, dt=F32):
            return ctx.enter_context(nc.sbuf_tensor(name, shape, dt))

        def sem(name):
            return ctx.enter_context(nc.semaphore(name))

        bank = [ctx.enter_context(nc.psum_tensor(f"bank{i}", [P, 512], F32)) for i in range(8)]

        X = sb("X", [P, NB * T])
        X1 = sb("X1", [P, NB * T])
        W = {}
        for k, v in w.items():
            if k == "bias_rows":
                W[k] = sb("w_" + k, [3, v.shape[1]])
            elif k == "rows":
                W[k] = sb("w_" + k, [P, v.shape[1]])
            else:
                W[k] = sb("w_" + k, list(v.shape), v.dtype)
        ident = W["c_ident"]
        identb, mask_tiles = W["c_identb"].bitcast(BF16), W["c_masks"].bitcast(BF16)
        NBIAS = NE * C + C
        bias_parts = sb("bias_parts", [3, NBIAS], BF16)
        b2_rows = sb("b2_rows", [3, NE * 4 * C], BF16)
        ones3 = sb("ones3", [3, P], BF16)
        ones = sb("ones", [P, P])
        power = sb("power", [P, 4])
        a_neg = sb("a_neg", [P, MH])
        d_quarter = sb("d_quarter", [P, MH])

        st = sb("st", [P, 4, 6])
        mv = sb("mv", [P, 4, 2])
        rs = sb("rs", [P, 8, 4])
        XN = sb("XN", [P, 4 * P])
        HT = sb("HT", [P, 2, 512])
        lst = sb("lst", [P, 2, 6])
        lmv = sb("lmv", [P, 2, 2])
        lrs = sb("lrs", [P, 2, 2])
        LN = sb("LN", [P, 2, LAT])
        LT = sb("LT", [LAT, T])
        roped = sb("roped", [P, 2, 512])
        RT = sb("RT", [P, 3, T])
        QKVG = sb("QKVG", [3 * HD * G, H * 64])
        VT = sb("VT", [P, T])
        rest = sb("rest", [P, 2, T])
        parts = sb("parts", [P, 2, 3, T], BF16)
        q_tiles = [sb(f"q_tile{i}", [P, H * T], BF16) for i in range(3)]
        k_tiles = [sb(f"k_tile{i}", [P, H * T], BF16) for i in range(3)]
        VP = [sb(f"VP{i}", [P, NT * H * VPITCH], BF16) for i in range(3)]
        v_left = sb("v_left", [P, T])
        NM = sb("NM", [P, 3, H, 2])
        nm_rest = sb("nm_rest", [P, 2 * H])
        NMP = sb("NMP", [P, 3, 2 * H], BF16)
        NMT = sb("NMT", [6 * H, P], BF16)
        PR = sb("PR", [P, 4, 512])
        PH = sb("PH", [P, 4, 512], F16)
        PL = sb("PL", [P, 4, 512], F16)
        YS = sb("YS", [P, NT * H * HD])
        YO = sb("YO", [P, NT * H * HD])
        rec = sb("rec", [P, NT * H])
        exp_shift = sb("exp_shift", [P, 1])
        YT = sb("YT", [P, T])

        bias_r = HT[0:3, :, :].rearrange("p a t -> p (a t)")[:, 0:NBIAS]
        bias_hi = XN[0:3, 0:NBIAS // 2].bitcast(BF16)
        bias_mid = QKVG[0:3, 0:NBIAS // 2].bitcast(BF16)

        LG = sb("LG", [P, 16])
        gmax = sb("gmax", [P, 2, 4])
        geq = sb("geq", [P, 2, 16])
        OH = sb("OH", [P, 2, 16])
        HID = [q[:, :].bitcast(F32).rearrange("p (c t) -> p c t", c=HC) for q in q_tiles[0:2]]
        YE = sb("YE", [P, 2, 512])

        part_dram = nc.dram_tensor("part_dram", (3, 2, 3, HD, H, T), BF16).ap()
        a_dram = nc.dram_tensor("a_dram", (3, H, 3 * HD * G, 64), F32).ap()

        names = """settled ones_rows early_loaded rest_loaded x_loaded x_rest_loaded const_set v_ones bias_split
            scores_ready score_maxed max_split max_T max_rows
            st_ready exp_hi exps_done exp_lo_dve exp_lo_pool pv_done y_summed y_normed y_T y_T_copied y_projected resid_added
            x_bn x_moments rstd_steps x_normed xT_ready hT_ready
            lat_ready q_ready lat_bn lat_moments lat_rstd lat_normed latT_psum latT_ready k_ready v_ready
            rope_product roped_sum v_hi v_rest v_mid v_lo part_hi part_rest part_mid part_lo
            a_proj a_v_ordered a_v_T a_evac_act a_evac_dve
            e_bn e_moments e_rstd e_normed e_xT e_hT e_logits e_route e_acc
            hid_ready hid_act hid_dve ye_ready ye_masked ye_added out_done""".split()
        S = {n: sem(n) for n in names}
        parts_written = [sem(f"parts_written{i}") for i in range(3)]
        qk_packed = [sem(f"qk_packed{i}") for i in range(3)]
        maxrow_landed = [sem(f"maxrow_landed{i}") for i in range(3)]
        a_written = [sem(f"a_written{i}") for i in range(3)]
        a_loaded = [sem(f"a_loaded{i}") for i in range(3)]

        N_LOADS = len(w)
        EARLY = ("a_w", "a_b", "c_ident", "bias_rows", "c_part", "rows", "c_identb", "c_masks", "a_wo")
        FIRST_LOAD = 2
        POOL_UNITS = (1, 4, 7, 9, 11)
        Y_BANK = (5, 2)

        def xcols(b):
            return bass.ds(b.x * T, T)

        def xtile(b, t):
            return bass.ds(b.x * T + t * P, P)

        def tile_order(ap):
            return ap.rearrange("p (g x c) -> p x g c", g=G, x=NT)

        def settle(eng):
            eng.sem_inc(S["settled"], 1)

        def cnt(kind, b, a_per, m_per, k):
            if kind == "A":
                return b.x * a_per + k
            return NB * a_per + (b.n - NB) * m_per + k

        def dve_stats(dve, kind, b):
            if kind == "A" and isinstance(b.x, int) and b.x == FIRST_LOAD:
                dve.wait_ge(S["x_rest_loaded"], 16)
            if b.layer == 1 and isinstance(b.x, int) and b.x < 3:
                dve.wait_ge(S["resid_added"], b.x + 1)
            wait(dve, S["rstd_steps"], cnt(kind, b, 2, 7, 0))
            wait(dve, S["x_normed"], cnt(kind, b, 2, 4, 0))
            for t in range(NT):
                dve.bn_stats(st[:, t, :], X[:, xtile(b, t)]).then_inc(S["x_bn"], 1)
            dve.wait_ge(S["x_bn"], b.n * 2 + 2)
            settle(dve)
            for t in range(NT):
                dve.bn_aggr(mv[:, t, :], st[:, t, :]).then_inc(S["x_moments"], 1)

        def dve_norm(dve, kind, b):
            dve.wait_ge(S["rstd_steps"], cnt(kind, b, 2, 7, 2 if kind == "A" else 7))
            wait(dve, S["xT_ready"], b.n)
            r = 1 if kind == "A" else 6
            for t in range(NT):
                dve.tensor_scalar(XN[:, t * P:(t + 1) * P], X[:, xtile(b, t)], mv[:, t, 0:1],
                                  rs[:, r, t:t + 1], ALU.subtract, ALU.mult).then_inc(S["x_normed"], 1)
            if kind == "M":
                for t in range(NT):
                    dve.tensor_scalar(X1[:, xtile(b, t)], X[:, xtile(b, t)], mv[:, t, 0:1],
                                      rs[:, 1, t:t + 1], ALU.subtract, ALU.mult).then_inc(S["x_normed"], 1)

        def dve_a_evac(dve, b):
            dve.wait_ge(S["a_proj"], b.x * 2 + 2)
            wait(dve, a_written[(b.m + 2) % 3], before_done(b, 16))
            for c in (2, 3):
                dve.tensor_scalar(QKVG[:, :].rearrange("p (t c) -> p c t", c=CL)[:, c, :],
                                  bank[6][0:96, (c - 2) * T:(c - 1) * T], W["a_b"][:, c:c + 1], None,
                                  ALU.add).then_inc(S["a_evac_dve"], 1)

        def dve_rope(dve, b, which):
            dve.wait_ge(S["q_ready" if which == 0 else "k_ready"], b.n - NB + 1)
            wait(dve, S["roped_sum"], (b.n - NB) * 2 + which)
            dve.tensor_tensor(roped[:, which, :], bank[7][:, :], W["c_rope"][:, :],
                              ALU.mult).then_inc(S["rope_product"], 1)
            dve.wait_ge(S["rope_product"], (b.n - NB) * 2 + which + 1)
            wait(dve, S["part_rest"], b.n * 2)
            wait(dve, S["part_hi"], b.n * 2)
            dve.tensor_tensor(RT[:, which, :], roped[:, which, 0:T], roped[:, which, T:2 * T],
                              ALU.add).then_inc(S["roped_sum"], 1)

        def dve_lat_stats(dve, b):
            n = b.n - NB
            dve.wait_ge(S["lat_ready"], n + 1)
            wait(dve, S["lat_rstd"], n * 2)
            wait(dve, S["lat_normed"], n * 2)
            for t in range(NT):
                dve.bn_stats(lst[:, t, :], bank[6][:, t * LAT:(t + 1) * LAT]).then_inc(S["lat_bn"], 1)
            dve.wait_ge(S["lat_bn"], n * 2 + 2)
            settle(dve)
            for t in range(NT):
                dve.bn_aggr(lmv[:, t, :], lst[:, t, :]).then_inc(S["lat_moments"], 1)

        def dve_lat_norm(dve, b):
            n = b.n - NB
            dve.wait_ge(S["lat_rstd"], n * 2 + 2)
            wait(dve, S["latT_psum"], n)
            for t in range(NT):
                dve.tensor_scalar(LN[:, t, :], bank[6][:, t * LAT:(t + 1) * LAT], lmv[:, t, 0:1],
                                  lrs[:, 1, t:t + 1], ALU.subtract, ALU.mult).then_inc(S["lat_normed"], 1)

        def split_source(kind, op):
            return tile_order(RT[:, op, :]) if kind == "A" else RT[:, op, :]

        def as_source(kind, ap):
            return ap.rearrange("p (x g c) -> p x g c", g=G, x=NT) if kind == "A" else ap

        def dve_split(dve, kind, b, op):
            dve.wait_ge(S["part_hi"], b.n * 2 + op + 1)
            wait(dve, S["part_lo"], b.n * 2)
            dve.tensor_tensor(as_source(kind, rest[:, op, :]), split_source(kind, op),
                              as_source(kind, parts[:, op, 0, :]), ALU.subtract).then_inc(S["part_rest"], 1)
            dve.wait_ge(S["part_rest"], b.n * 2 + op + 1)
            dve.tensor_copy(parts[:, op, 1, :], rest[:, op, :]).then_inc(S["part_mid"], 1)

        def dve_max(dve, b, u):
            dve.wait_ge(S["scores_ready"], b.n * UNITS + u + 1)
            if u == 0:
                wait(dve, S["max_split"], done(b, 3, 4))
            q, j = u // 3, u % 3
            src = bank[3 + u % 2]
            if j < 2:
                h = 4 * q + 2 * j
                dve.tensor_reduce(NM[:, b.m, h:h + 2, 1], src[:, :].rearrange("p (h k) -> p h k", h=2),
                                  AX.X, ALU.max, negate=True).then_inc(S["score_maxed"], 1)
            else:
                dve.tensor_reduce(NM[:, b.m, 4 * q:4 * q + 4, 0], src[:, :].rearrange("p (h k) -> p h k", h=4),
                                  AX.X, ALU.max, negate=True).then_inc(S["score_maxed"], 1)

        def dve_v_rest(dve, kind, b):
            dve.wait_ge(S["v_hi"], b.n + 1)
            wait(dve, S["v_lo"], b.n)
            src = bank[6 if kind == "M" else 7][:, 0:T].rearrange("p (m d) -> p m d", d=HD)
            left = v_left[:, :].rearrange("p (m d) -> p m d", d=HD)
            dve.tensor_tensor(left, src, v_part(b, 0), ALU.subtract).then_inc(S["v_rest"], 1)
            dve.wait_ge(S["v_rest"], b.n + 1)
            dve.tensor_copy(v_part(b, 1), left).then_inc(S["v_mid"], 1)

        def exp_lo(eng, b, u):
            eng.wait_ge(S["exps_done"], b.n * UNITS + u + 1)
            pool = eng is nc.gpsimd
            if pool:
                settle(eng)
            eng.tensor_tensor(PL[:, u % 4, :], PR[:, u % 4, :], PH[:, u % 4, :],
                              ALU.subtract).then_inc(S["exp_lo_pool" if pool else "exp_lo_dve"], 1)

        def wait_exp_lo(eng, b, u):
            mine = [v for v in range(UNITS) if (v in POOL_UNITS) == (u in POOL_UNITS)]
            eng.wait_ge(S["exp_lo_pool" if u in POOL_UNITS else "exp_lo_dve"], b.n * len(mine) + mine.index(u) + 1)

        def dve_y(dve, b):
            dve.wait_ge(S["pv_done"], (b.n + 1) * UNITS)
            wait(dve, S["y_normed"], b.n)
            for t in range(NT):
                src = bank[Y_BANK[t]][:, 0:H * VPITCH].rearrange("p (h c) -> p h c", h=H)
                dve.tensor_reduce(YS[:, t * P:(t + 1) * P].rearrange("p (h d) -> p h d", h=H),
                                  src[:, :, 0:3 * HD].rearrange("p h (s d) -> p h d s", s=3),
                                  AX.X, ALU.add).then_inc(S["y_summed"], 1)
                dve.reciprocal(rec[:, t * H:(t + 1) * H], src[:, :, 3 * HD]).then_inc(S["y_summed"], 1)
            dve.wait_ge(S["y_summed"], b.n * 4 + 4)
            wait(dve, S["y_T"], b.n)
            dve.tensor_tensor(YO[:, :].rearrange("p (m d) -> p m d", d=HD),
                              YS[:, :].rearrange("p (m d) -> p m d", d=HD),
                              rec[:, :].unsqueeze(2).broadcast_to([P, NT * H, HD]),
                              ALU.mult).then_inc(S["y_normed"], 1)

        def dve_resid(dve, kind, b):
            dve.wait_ge(S["y_projected"], b.n + 1)
            dst = X if kind == "A" else X1
            dve.tensor_tensor(dst[:, xcols(b)], dst[:, xcols(b)], bank[6][:, T:2 * T],
                              ALU.add).then_inc(S["resid_added"], 1)

        def pool_rstd(pool, kind, b):
            pool.wait_ge(S["x_moments"], b.n * 2 + 2)
            s0 = cnt(kind, b, 2, 7, 0)
            wait(pool, S["x_normed"], cnt(kind, b, 2, 4, 0))
            rstd_chain(pool, S["rstd_steps"], s0, mv[:, 0:2, 1], rs, 2, kind != "A")

        def rstd_chain(pool, s, s0, var, rs, n, double):
            r = lambda k: rs[:, k, 0:n]
            settle(pool)
            pool.tensor_scalar(r(0), var, 1e-5, None, ALU.add).then_inc(s, 1)
            pool.wait_ge(s, s0 + 1)
            settle(pool)
            pool.tensor_tensor(r(1), r(0), power[:, 0:n], ALU.pow).then_inc(s, 1)
            if not double:
                return
            pool.wait_ge(s, s0 + 2)
            settle(pool)
            pool.tensor_tensor(r(2), r(1), r(1), ALU.mult).then_inc(s, 1)
            pool.wait_ge(s, s0 + 3)
            settle(pool)
            pool.tensor_tensor(r(3), r(2), var, ALU.mult).then_inc(s, 1)
            pool.wait_ge(s, s0 + 4)
            settle(pool)
            pool.tensor_scalar(r(4), r(3), 1e-6, None, ALU.add).then_inc(s, 1)
            pool.wait_ge(s, s0 + 5)
            settle(pool)
            pool.tensor_tensor(r(5), r(4), power[:, 0:n], ALU.pow).then_inc(s, 1)
            pool.wait_ge(s, s0 + 6)
            settle(pool)
            pool.tensor_tensor(r(6), r(5), r(1), ALU.mult).then_inc(s, 1)

        def pool_lat_rstd(pool, b):
            n = b.n - NB
            pool.wait_ge(S["lat_moments"], n * 2 + 2)
            wait(pool, S["lat_normed"], n * 2)
            settle(pool)
            pool.tensor_scalar(lrs[:, 0, :], lmv[:, :, 1], 1e-5, None, ALU.add).then_inc(S["lat_rstd"], 1)
            pool.wait_ge(S["lat_rstd"], n * 2 + 1)
            settle(pool)
            pool.tensor_tensor(lrs[:, 1, :], lrs[:, 0, :], power[:, 0:2], ALU.pow).then_inc(S["lat_rstd"], 1)

        def pool_split(pool, b, op):
            pool.wait_ge(S["part_mid"], b.n * 2 + op + 1)
            wait(pool, parts_written[(b.m + 2) % 3], before_done(b, 96))
            settle(pool)
            pool.tensor_tensor(parts[:, op, 2, :], rest[:, op, :], parts[:, op, 1, :],
                               ALU.subtract).then_inc(S["part_lo"], 1)

        def pool_v_lo(pool, b):
            pool.wait_ge(S["v_mid"], b.n + 1)
            settle(pool)
            pool.tensor_tensor(v_part(b, 2), v_left[:, :].rearrange("p (m d) -> p m d", d=HD), v_part(b, 1),
                               ALU.subtract).then_inc(S["v_lo"], 1)

        def pool_a_v(pool, b):
            pool.wait_ge(a_loaded[b.m], b.use * 48 + 48)
            wait(pool, S["a_v_T"], b.x)
            settle(pool)
            pool.tensor_copy(VT[:, :].rearrange("p (x g c) -> p x g c", g=G, x=NT),
                             tile_order(RT[:, 2, :])).then_inc(S["a_v_ordered"], 1)

        def pool_max_split(pool, b):
            nm = NM[:, b.m, :, :].rearrange("p h x -> p (h x)")
            pool.wait_ge(S["score_maxed"], (b.n + 1) * UNITS)
            wait(pool, S["max_T"], b.n)
            settle(pool)
            pool.tensor_copy(NMP[:, 0, :], nm).then_inc(S["max_split"], 1)
            pool.wait_ge(S["max_split"], b.n * 4 + 1)
            settle(pool)
            pool.tensor_tensor(nm_rest[:, :], nm, NMP[:, 0, :], ALU.subtract).then_inc(S["max_split"], 1)
            pool.wait_ge(S["max_split"], b.n * 4 + 2)
            settle(pool)
            pool.tensor_copy(NMP[:, 1, :], nm_rest[:, :]).then_inc(S["max_split"], 1)
            pool.wait_ge(S["max_split"], b.n * 4 + 3)
            settle(pool)
            pool.tensor_tensor(NMP[:, 2, :], nm_rest[:, :], NMP[:, 1, :], ALU.subtract).then_inc(S["max_split"], 1)

        def act_hT(act, kind, b):
            act.wait_ge(S["xT_ready"], b.n + 1)
            if kind == "A":
                wait(act, S["a_proj"], b.x * 2)
                act.activation(HT[:, 0, 0:T], bank[6][:, 0:T], ACT.Copy).then_inc(S["hT_ready"], 1)
            else:
                if isinstance(b.x, int) and b.x == 0:
                    act.wait_ge(S["a_proj"], NB * 2)
                wait(act, S["q_ready"], b.n - NB)
                act.activation(HT[:, 0, 0:T], bank[6][:, 0:T], ACT.Identity,
                               scale=W["cols"][:, 0:1]).then_inc(S["hT_ready"], 1)

        def act_a_evac(act, b):
            act.wait_ge(S["a_proj"], b.x * 2 + 1)
            wait(act, a_written[(b.m + 2) % 3], before_done(b, 16))
            for c in (0, 1):
                act.activation(QKVG[:, :].rearrange("p (t c) -> p c t", c=CL)[:, c, :],
                               bank[7][0:96, c * T:(c + 1) * T], ACT.Identity,
                               bias=W["a_b"][:, c:c + 1]).then_inc(S["a_evac_act"], 1)

        def act_latT(act, b):
            n = b.n - NB
            act.wait_ge(S["latT_psum"], n + 1)
            wait(act, S["v_ready"], n)
            act.activation(LT[:, :], bank[6][0:LAT, 0:T], ACT.Identity, scale=W["lat_cols"][:, 0:1],
                           bias=W["lat_cols"][:, 1:2]).then_inc(S["latT_ready"], 1)

        def act_v(act, kind, b):
            act.wait_ge(S["v_ready"] if kind == "M" else S["a_v_T"], (b.n - NB if kind == "M" else b.x) + 1)
            wait(act, S["pv_done"], done(b, 3, UNITS))
            src = bank[6 if kind == "M" else 7][:, 0:T].rearrange("p (m d) -> p m d", d=HD)
            act.activation(v_part(b, 0), src, ACT.Copy).then_inc(S["v_hi"], 1)

        def act_split(act, kind, b, op):
            if kind == "A":
                act.wait_ge(a_loaded[b.m], b.use * 48 + 48)
            else:
                act.wait_ge(S["roped_sum"], (b.n - NB) * 2 + op + 1)
            wait(act, parts_written[(b.m + 2) % 3], before_done(b, 96))
            wait(act, S["part_rest"], b.n * 2)
            act.activation(as_source(kind, parts[:, op, 0, :]), split_source(kind, op),
                           ACT.Copy).then_inc(S["part_hi"], 1)

        def act_max_rows(act, b):
            act.wait_ge(S["max_T"], b.n + 1)
            wait(act, maxrow_landed[(b.m + 2) % 3], before_done(b, 16))
            act.activation(NMT[:, :], bank[7][0:6 * H, 0:P // 2].bitcast(BF16),
                           ACT.Copy).then_inc(S["max_rows"], 1)
            act.wait_ge(S["max_rows"], b.n + 1)
            act.dma_start(q_tiles[b.m][KQ:KM, :].rearrange("p (n t) -> p n t", t=P),
                          NMT[:, :]).then_inc(maxrow_landed[b.m], 16)

        def act_exp(act, b, u):
            act.wait_ge(S["st_ready"], b.n * UNITS + u + 1)
            wait(act, S["pv_done"], b.n * UNITS + u - 3)
            act.activation(PH[:, u % 4, :], bank[u % 2][:, :], ACT.Exp, bias=exp_shift[:, :],
                           scale=SCALE).then_inc(S["exp_hi"], 1)
            act.activation(PR[:, u % 4, :], bank[u % 2][:, :], ACT.Exp, bias=exp_shift[:, :],
                           scale=SCALE).then_inc(S["exps_done"], 1)

        def act_y_T(act, kind, b):
            act.wait_ge(S["y_T"], b.n + 1)
            wait(act, S["y_projected"], b.n)
            for t in range(NT):
                src, dst = bank[6][:, T + t * P:T + (t + 1) * P], YT[:, t * P:(t + 1) * P]
                if kind == "A":
                    src = src.rearrange("p (g r c) -> p g r c", g=G, c=CL)
                    dst = dst.rearrange("p (r g c) -> p g r c", g=G, c=CL)
                act.activation(dst, src, ACT.Copy).then_inc(S["y_T_copied"], 1)

        def pe_T(pe, kind, b):
            pe.wait_ge(S["x_normed"], cnt(kind, b, 2, 4, 2))
            bank6_free(pe, kind, b)
            for t in range(NT):
                mm = pe.transpose(bank[6][:, t * P:(t + 1) * P], XN[:, t * P:(t + 1) * P], ident[:, :])
            mm.then_inc(S["xT_ready"], 1)

        def bank6_free(pe, kind, b):
            if kind == "A":
                wait(pe, S["a_evac_dve"], b.x * 2)
            else:
                wait(pe, S["v_rest"], b.n)
            wait(pe, S["resid_added"], done(b, 4, 1))

        def pe_a_proj(pe, b):
            pe.wait_ge(S["hT_ready"], b.n + 1)
            wait(pe, S["v_rest"], b.n)

            for c in range(CL):
                mm = pe.matmul(bank[7 if c < 2 else 6][0:96, (c % 2) * T:(c % 2 + 1) * T],
                               W["a_w"][:, c * 96:(c + 1) * 96], HT[:, 0, 0:T], start=True, stop=True)
                if c % 2:
                    mm.then_inc(S["a_proj"], 1)

        def pe_a_v(pe, b):
            pe.wait_ge(S["a_v_ordered"], b.x + 1)
            pe.wait_ge(S["a_evac_act"], b.x * 2 + 2)
            wait(pe, S["max_rows"], done(b, 2, 1))
            for t in range(NT):
                mm = pe.transpose(bank[7][:, t * P:(t + 1) * P], VT[:, t * P:(t + 1) * P], ident[:, :])
            mm.then_inc(S["a_v_T"], 1)

        def pe_qlat(pe, b):
            n = b.n - NB
            pe.wait_ge(S["hT_ready"], b.n + 1)
            for t in range(NT):
                mm = pe.matmul(bank[6][:, t * LAT:(t + 1) * LAT], HT[:, 0, t * P:(t + 1) * P],
                               W["m_wdkv"][:, :], start=True, stop=True)
            mm.then_inc(S["lat_ready"], 1)
            wait(pe, S["rope_product"], n * 2)
            for r in range(2):
                mm = pe.matmul(bank[7][:, r * T:(r + 1) * T], W["m_wq"][:, r * P:(r + 1) * P], HT[:, 0, 0:T],
                               start=True, stop=True)
            mm.then_inc(S["q_ready"], 1)

        def pe_latT(pe, b):
            n = b.n - NB
            pe.wait_ge(S["lat_normed"], n * 2 + 2)
            settle(pe)
            for t in range(NT):
                mm = pe.transpose(bank[6][0:LAT, t * P:(t + 1) * P], LN[:, t, :], ident[:, :])
            mm.then_inc(S["latT_psum"], 1)

        def pe_kv(pe, b):
            n = b.n - NB
            pe.wait_ge(S["latT_ready"], n + 1)
            pe.wait_ge(S["rope_product"], n * 2 + 1)
            wait(pe, S["max_rows"], done(b, 2, 1))
            for r in range(2):
                mm = pe.matmul(bank[7][:, r * T:(r + 1) * T], W["m_wuk"][:, r * P:(r + 1) * P], LT[:, :],
                               start=True, stop=True)
            mm.then_inc(S["k_ready"], 1)
            for t in range(NT):
                mm = pe.matmul(bank[6][:, t * P:(t + 1) * P], LT[:, t * P:(t + 1) * P], W["m_wuv"][:, :],
                               start=True, stop=True)
            mm.then_inc(S["v_ready"], 1)

        def score_unit(pe, b, u, keys_out, mask, rows, dst, ready):
            q, j = u // 3, u % 3
            qp = q_tiles[b.m][0:rows, :].rearrange("p (h t) -> p h t", h=H)
            kp = k_tiles[b.m][0:rows, :].rearrange("p (h t) -> p h t", h=H)
            lhs, rhs = (kp, qp) if keys_out else (qp, kp)
            full, alone = (0, 1) if keys_out else (1, 0)
            pe.matmul(dst[:, :], identb[:, :], mask[:, (0 if j < 2 else 512):(512 if j < 2 else 1024)],
                      start=True, stop=False, skip_group_check=True)
            if j < 2:
                for i in range(2):
                    h = 4 * q + 2 * j + i
                    mm = pe.matmul(dst[:, i * T:(i + 1) * T], lhs[:, h, full * P:(full + 1) * P], rhs[:, h, :],
                                   start=False, stop=(i == 1), skip_group_check=True)
            else:
                for i in range(4):
                    h = 4 * q + i
                    mm = pe.matmul(dst[:, i * P:(i + 1) * P], lhs[:, h, alone * P:(alone + 1) * P],
                                   rhs[:, h, alone * P:(alone + 1) * P], start=False, stop=(i == 3),
                                   skip_group_check=True)
            mm.then_inc(ready, 1)

        def masks(kind, keys_out):
            i = (0 if kind == "A" else 2) + keys_out
            return mask_tiles[:, i * 1024:(i + 1) * 1024]

        def pe_s(pe, kind, b, u):
            if u == 0:
                pe.wait_ge(qk_packed[b.m], b.use * 96 + 96)
            wait(pe, S["score_maxed"], b.n * UNITS + u - 1)
            score_unit(pe, b, u, 0, masks(kind, 0), KQ, bank[3 + u % 2], S["scores_ready"])

        def rope_count(b, ahead):
            n = (b.layer - 1) * NB
            if isinstance(b.x, int) and b.x + ahead >= NB:
                return (n + NB) * 2
            return (b.x + ahead + n) * 2 + 1

        def pe_max_T(pe, kind, b):
            pe.wait_ge(S["max_split"], b.n * 4 + 4)
            wait(pe, S["max_rows"], b.n)
            if kind == "A":
                pe.wait_ge(S["a_evac_act"], min2(b.x + 3, NB) * 2)
                if isinstance(b.x, int) and b.x + 2 >= NB:
                    pe.wait_ge(S["rope_product"], (b.x + 2 - NB) * 2 + 1)
            else:
                pe.wait_ge(S["rope_product"], rope_count(b, 2))
            pe.transpose(bank[7][0:6 * H, 0:P // 2].bitcast(BF16),
                         NMP[:, :, :].rearrange("p a n -> p (a n)"), identb[:, :]).then_inc(S["max_T"], 1)

        def pe_st(pe, kind, b, u):
            if u == 0:
                pe.wait_ge(maxrow_landed[b.m], b.use * 16 + 16)
            wait(pe, S["exps_done"], b.n * UNITS + u - 1)
            score_unit(pe, b, u, 1, masks(kind, 1), KM, bank[u % 2], S["st_ready"])

        def v_part(b, i):
            return VP[b.m][:, :].rearrange("p (m c) -> p m c", c=VPITCH)[:, :, i * HD:(i + 1) * HD]

        def pe_pv(pe, b, u):
            if u == 0:
                pe.wait_ge(S["v_lo"], b.n + 1)
                wait(pe, S["y_summed"], b.n * 4)
            q, j = u // 3, u % 3

            def product(probs, cols, key_tile, h, query_tile, first=False):
                v = (key_tile * H + h) * VPITCH
                return pe.matmul(bank[Y_BANK[query_tile]][:, h * VPITCH:h * VPITCH + VW],
                                 probs[:, u % 4, cols * P:(cols + 1) * P], VP[b.m][:, v:v + VW],
                                 start=first, stop=False, skip_group_check=True)
            for probs in (PH, PL):
                if probs is PH:
                    pe.wait_ge(S["exp_hi"], b.n * UNITS + u + 1)
                else:
                    wait_exp_lo(pe, b, u)
                first = u == 0 and probs is PH
                if j < 2:
                    for i in range(2):
                        for t in range(NT):
                            mm = product(probs, 2 * i + t, 0, 4 * q + 2 * j + i, t, first and i == 0)
                else:
                    for i in range(4):
                        mm = product(probs, i, 1, 4 * q + i, 1)
            mm.then_inc(S["pv_done"], 1)

        def pe_y_T(pe, kind, b):
            pe.wait_ge(S["y_normed"], b.n + 1)
            if kind == "A":
                pe.wait_ge(S["a_evac_dve"], min2(b.x + 4, NB) * 2)
                if isinstance(b.x, int) and b.x + 3 >= NB:
                    pe.wait_ge(S["v_rest"], b.n + 4)
            else:
                pe.wait_ge(S["v_rest"], b.layer * NB + min2(b.x + 4, NB))
            wait(pe, S["resid_added"], b.n)
            for t in range(NT):
                mm = pe.transpose(bank[6][:, T + t * P:T + (t + 1) * P], YO[:, t * P:(t + 1) * P], ident[:, :])
            mm.then_inc(S["y_T"], 1)

        def pe_project(pe, kind, b):
            pe.wait_ge(S["y_T_copied"], b.n * 2 + 2)
            for t in range(NT):
                dst = bank[6][:, T + t * P:T + (t + 1) * P]
                if kind == "A":
                    pe.matmul(dst, ones3[:, :], bias_parts[:, NE * C:], start=(t == 0),
                              stop=False, skip_group_check=True)
                mm = pe.matmul(dst, YT[:, t * P:(t + 1) * P],
                               W["a_wo" if kind == "A" else "m_wo"][:, :], start=(kind != "A" and t == 0),
                               stop=True, skip_group_check=True)
            mm.then_inc(S["y_projected"], 1)

        def min2(a, b):
            return min(a, b) if isinstance(a, int) else a

        def before_done(b, per):
            if isinstance(b.n, int) and b.n < 1:
                return None
            return b.use_before * per + per

        def sp_a(sp, b):
            sp.wait_ge(S["a_evac_act"], b.x * 2 + 2)
            sp.wait_ge(S["a_evac_dve"], b.x * 2 + 2)
            sp.dma_start(a_dram[b.m].rearrange("h r t -> r h t"),
                         QKVG[:, :].rearrange("r (h t) -> r h t", h=H)).then_inc(a_written[b.m], 16)
            sp.wait_ge(a_written[b.m], b.use * 16 + 16)
            wait(sp, S["part_rest"], b.n * 2)
            wait(sp, S["a_v_T"], b.x)
            src = a_dram[b.m].rearrange("h (o d g) t -> o h d (g t)", o=3, g=G)
            for op in range(3):
                sp.dma_start(RT[:, op, :], src[op]).then_inc(a_loaded[b.m], 16)

        def sp_parts(sp, b, op):
            sp.wait_ge(S["part_lo"], b.n * 2 + op + 1)
            for i in range(3):
                sp.dma_start(part_dram[b.m, op, i].rearrange("d h t -> h d t"),
                             parts[:, op, i, :]).then_inc(parts_written[b.m], 16)

        def sp_pack(sp, b):
            sp.wait_ge(parts_written[b.m], b.use * 96 + 96)
            settle(sp)
            wait(sp, S["st_ready"], done(b, 3, UNITS))
            settle(sp)
            flat = part_dram[b.m].rearrange("o i d h t -> o i d (h t)")
            for i in range(3):
                rows = slice(i * 3 * HD, (i + 1) * 3 * HD)
                sp.dma_start(q_tiles[b.m][rows, :],
                             flat[0, i:i + 1].broadcast_to([3, HD, H * T])).then_inc(qk_packed[b.m], 16)
                sp.dma_start(k_tiles[b.m][rows, :], flat[1, 0:3]).then_inc(qk_packed[b.m], 16)

        def attention_slot(at):
            prelude = {} if at(0) is None else PRELUDE["A" if at(0).layer == 0 else "M"]
            order = []

            def add(step, d, u=0):
                if at(d) is not None:
                    order.append((step, at(d), u))

            def unit(step, g, d):
                add(step, d if g >= 0 else d + 1, g % UNITS)
            for u in range(UNITS):
                unit("st", u - EX, 2)
                unit("lo", u - EX - LO_LAG, 2)
                if u == EX + PV_LAG:
                    add("y", 3)
                for step, d in OTHERS.get(u, ()):
                    add(step, d)
                for step in prelude.get(u, ()):
                    add(step, 0)
                unit("s", u - S_AT, 1)
                if u == S_AT - 1:
                    add("max", 2)
                g = u - EX - PV_LAG
                if g == 1:
                    unit("pv", 0, 2)
                if g != 0:
                    unit("pv", g, 2)
                for step, d in LATE.get(u, ()):
                    add(step, d)
            return order

        EX, S_AT = 7, 3
        LO_LAG, PV_LAG = 1, 2
        OTHERS = {4: [("max_T", 2)]}
        LATE = {10: [("y_T", 3)], 11: [("project", 3)]}
        PRELUDE = {"M": {0: ["stats"], 1: ["norm"], 3: ["T", "proj"], 4: ["latnorm"], 5: ["hi0"],
                         6: ["split0", "latT"], 8: ["kv", "hi1"], 9: ["split1", "pack"]},
                   "A": {0: ["stats"], 1: ["norm"], 2: ["T"], 3: ["proj"], 7: ["order_v"], 8: ["hi0"],
                         9: ["split0", "hi1", "split1", "pack"], 10: ["kv"]}}

        def attention(eng, part, layer):
            def slot(it, c):
                def at(d):
                    if it is None and not 0 <= c - d < NB:
                        return batch(1, None, c - d - NB, 3) if layer == 0 and c - d >= NB else None
                    return batch(layer, it, c - d, 3)
                for step, b, u in attention_slot(at):
                    part(eng, "A" if b.layer == 0 else "M", step, b, u)
            start = {0: 0, 1: 3, 2: 0}[layer]
            loop = {0: 6, 1: 3, 2: 3}[layer]
            if layer == 1:
                eng.wait_ge(S["resid_added"], NB)
            for c in range(start, loop):
                if layer == 0 and c == FIRST_LOAD:
                    eng.wait_ge(S["rest_loaded"], 16 * (N_LOADS - len(EARLY)))
                slot(None, c)
            with eng.Fori(0, (NB - 1 - loop) // 3) as it:
                for c in range(loop, loop + 3):
                    slot(it, c)
            for c in range(NB - 1, NB + 3):
                slot(None, c)

        def dve_part(dve, kind, step, b, u):
            if step == "stats":
                dve_stats(dve, kind, b)
            elif step == "norm":
                dve_norm(dve, kind, b)
            elif step == "proj" and kind == "A":
                dve_a_evac(dve, b)
            elif step == "proj":
                dve_lat_stats(dve, b)
                dve_rope(dve, b, 0)
            elif step == "latnorm" and kind == "M":
                dve_lat_norm(dve, b)
            elif step == "kv":
                if kind == "M":
                    dve_rope(dve, b, 1)
                dve_v_rest(dve, kind, b)
            elif step == "lo" and u not in POOL_UNITS:
                exp_lo(dve, b, u)
            elif step in ("split0", "split1"):
                dve_split(dve, kind, b, int(step[-1]))
            elif step == "s":
                dve_max(dve, b, u)
            elif step == "y":
                dve_y(dve, b)
            elif step == "project":
                dve_resid(dve, kind, b)

        def pool_part(pool, kind, step, b, u):
            if step == "stats":
                pool_rstd(pool, kind, b)
            elif step == "proj" and kind == "M":
                pool_lat_rstd(pool, b)
            elif step == "kv":
                pool_v_lo(pool, b)
            elif step == "order_v":
                pool_a_v(pool, b)
            elif step in ("split0", "split1"):
                pool_split(pool, b, int(step[-1]))
            elif step == "max":
                pool_max_split(pool, b)
            elif step == "lo" and u in POOL_UNITS:
                exp_lo(pool, b, u)

        def act_part(act, kind, step, b, u):
            if step == "T":
                act_hT(act, kind, b)
            elif step == "proj" and kind == "A":
                act_a_evac(act, b)
            elif step == "latT" and kind == "M":
                act_latT(act, b)
            elif step == "kv":
                act_v(act, kind, b)
            elif step in ("hi0", "hi1"):
                act_split(act, kind, b, int(step[-1]))
            elif step == "max_T":
                act_max_rows(act, b)
            elif step == "st":
                act_exp(act, b, u)
            elif step == "y_T":
                act_y_T(act, kind, b)

        def pe_part(pe, kind, step, b, u):
            if step == "T":
                pe_T(pe, kind, b)
            elif step == "proj":
                pe_a_proj(pe, b) if kind == "A" else pe_qlat(pe, b)
            elif step == "latT" and kind == "M":
                pe_latT(pe, b)
            elif step == "kv":
                pe_a_v(pe, b) if kind == "A" else pe_kv(pe, b)
            elif step == "s":
                pe_s(pe, kind, b, u)
            elif step == "max_T":
                pe_max_T(pe, kind, b)
            elif step == "st":
                pe_st(pe, kind, b, u)
            elif step == "pv":
                pe_pv(pe, b, u)
            elif step == "y_T":
                pe_y_T(pe, kind, b)
            elif step == "project":
                pe_project(pe, kind, b)

        def sp_part(sp, kind, step, b, u):
            if step == "proj" and kind == "A":
                sp_a(sp, b)
            elif step in ("split0", "split1"):
                sp_parts(sp, b, int(step[-1]))
            elif step == "pack":
                sp_pack(sp, b)

        NU = NB // 2
        HID_BANK = (0, 1, 2, 5)

        def e_cols(b, t=None):
            return bass.ds(b.x * 2 * T, 2 * T) if t is None else bass.ds(b.x * 2 * T + t * P, P)

        def dve_e_stats(dve, b):
            wait(dve, S["e_rstd"], b.n * 4)
            for t in range(4):
                dve.bn_stats(st[:, t, :], X1[:, e_cols(b, t)]).then_inc(S["e_bn"], 1)
            dve.wait_ge(S["e_bn"], b.n * 4 + 4)
            settle(dve)
            for t in range(4):
                dve.bn_aggr(mv[:, t, :], st[:, t, :]).then_inc(S["e_moments"], 1)

        def pool_e_rstd(pool, b):
            s, v = S["e_rstd"], b.n * 4
            pool.wait_ge(S["e_moments"], v + 4)
            wait(pool, S["e_normed"], v)
            settle(pool)
            pool.tensor_tensor(rs[:, 0, :], mv[:, :, 0], mv[:, :, 0], ALU.mult).then_inc(s, 1)
            pool.wait_ge(s, v + 1)
            settle(pool)
            pool.tensor_tensor(rs[:, 1, :], rs[:, 0, :], mv[:, :, 1], ALU.add).then_inc(s, 1)
            pool.wait_ge(s, v + 2)
            settle(pool)
            pool.tensor_scalar(rs[:, 2, :], rs[:, 1, :], 1e-6, None, ALU.add).then_inc(s, 1)
            pool.wait_ge(s, v + 3)
            settle(pool)
            pool.tensor_tensor(rs[:, 3, :], rs[:, 2, :], power[:, :], ALU.pow).then_inc(s, 1)
            pool.tensor_tensor(X[:, e_cols(b)], X[:, e_cols(b)], X1[:, e_cols(b)], ALU.add).then_inc(S["e_acc"], 1)

        def dve_e_norm(dve, b):
            dve.wait_ge(S["e_rstd"], b.n * 4 + 4)
            wait(dve, S["e_xT"], b.n)
            for t in range(4):
                dve.tensor_scalar(XN[:, t * P:(t + 1) * P], X1[:, e_cols(b, t)], rs[:, 3, t:t + 1], None,
                                  ALU.mult).then_inc(S["e_normed"], 1)

        def pe_e_T(pe, b):
            pe.wait_ge(S["e_normed"], b.n * 4 + 4)
            wait(pe, S["e_hT"], b.n)
            for t in range(4):
                mm = pe.transpose(bank[6][:, t * P:(t + 1) * P], XN[:, t * P:(t + 1) * P], ident[:, :])
            mm.then_inc(S["e_xT"], 1)

        def act_e_hT(act, b):
            act.wait_ge(S["e_xT"], b.n + 1)
            wait(act, S["hid_ready"], done(b, 2, NE * HC))
            act.activation(HT[:, b.m, :], bank[6][:, :], ACT.Identity,
                           scale=W["cols"][:, 1:2]).then_inc(S["e_hT"], 1)

        def pe_e_gate(pe, b):
            pe.wait_ge(S["e_hT"], b.n + 1)
            wait(pe, S["e_route"], b.n * 6)
            for t in range(4):
                mm = pe.matmul(bank[7][:, t * NE:(t + 1) * NE], HT[:, b.m, t * P:(t + 1) * P], W["e_gate"][:, :],
                               start=True, stop=True)
            mm.then_inc(S["e_logits"], 1)

        def dve_e_route(dve, b):
            s, v = S["e_route"], b.n * 6
            grp = lambda ap: ap.rearrange("p (t e) -> p t e", e=NE)
            wide = lambda ap: ap.unsqueeze(2).broadcast_to([P, 4, NE])
            dve.wait_ge(S["e_logits"], b.n + 1)
            wait(dve, S["ye_masked"], done(b, 2, NE))
            dve.tensor_tensor(LG[:, :], bank[7][:, 0:16], W["rows"][:, 0:16], ALU.add).then_inc(s, 1)
            dve.wait_ge(s, v + 1)
            dve.tensor_reduce(gmax[:, 0, :], grp(LG[:, :]), AX.X, ALU.max).then_inc(s, 1)
            dve.wait_ge(s, v + 2)
            dve.tensor_tensor(grp(geq[:, 0, :]), grp(LG[:, :]), wide(gmax[:, 0, :]), ALU.is_equal).then_inc(s, 1)
            dve.wait_ge(s, v + 3)
            dve.tensor_tensor(geq[:, 1, :], geq[:, 0, :], W["c_rank"][:, :], ALU.mult).then_inc(s, 1)
            dve.wait_ge(s, v + 4)
            dve.tensor_reduce(gmax[:, 1, :], grp(geq[:, 1, :]), AX.X, ALU.max).then_inc(s, 1)
            dve.wait_ge(s, v + 5)
            dve.tensor_tensor(grp(OH[:, b.m, :]), grp(geq[:, 1, :]), wide(gmax[:, 1, :]), ALU.is_equal).then_inc(s, 1)

        def pe_e_hid(pe, b, e):
            if e == 0:
                pe.wait_ge(S["e_hT"], b.n + 1)
            for i in range(HC):
                c = e * HC + i
                wait(pe, S["hid_act" if c % 2 == 0 else "hid_dve"], b.n * (NE * HC // 2) + (c - 4) // 2 + 1)
                pe.matmul(bank[HID_BANK[c % 4]][:, :], W["e_w1"][:, c * P:(c + 1) * P], HT[:, b.m, :],
                          start=True, stop=True).then_inc(S["hid_ready"], 1)

        def e_evac(eng, b, e, odd):
            for i in range(odd, HC, 2):
                c = e * HC + i
                eng.wait_ge(S["hid_ready"], b.n * NE * HC + c + 1)
                wait(eng, S["ye_ready"], b.n * NE + e - 1)
                src, dst, bias = bank[HID_BANK[c % 4]][:, :], HID[e % 2][:, i, :], W["e_b1"][:, c:c + 1]
                if odd:
                    eng.tensor_scalar(dst, src, bias, 0.0, ALU.add, ALU.max).then_inc(S["hid_dve"], 1)
                else:
                    eng.activation(dst, src, ACT.Relu, bias=bias).then_inc(S["hid_act"], 1)

        def pe_e_y(pe, b, e):
            v = b.n * 8 + 2 * e + 2
            pe.wait_ge(S["hid_act"], v)
            pe.wait_ge(S["hid_dve"], v)
            wait(pe, S["ye_masked"], b.n * NE + e - 1)
            dst = bank[3 + e % 2]
            pe.matmul(dst[:, :], ones3[:, :], b2_rows[:, e * 4 * C:(e + 1) * 4 * C], start=True, stop=False,
                      skip_group_check=True)
            for t in range(4):
                for i in range(HC):
                    c = e * HC + i
                    mm = pe.matmul(dst[:, t * P:(t + 1) * P], HID[e % 2][:, i, t * P:(t + 1) * P],
                                   W["e_w2"][:, c * P:(c + 1) * P], start=False, stop=(i == HC - 1),
                                   skip_group_check=True)
            mm.then_inc(S["ye_ready"], 1)

        def dve_e_mask(dve, b, e):
            dve.wait_ge(S["ye_ready"], b.n * NE + e + 1)
            if e == 0:
                dve.wait_ge(S["e_route"], b.n * 6 + 6)
            wait(dve, S["ye_added"], b.n * NE + e - 1)
            oh = OH[:, b.m, :].rearrange("p (t e) -> p t e", e=NE)[:, :, e:e + 1].broadcast_to([P, 4, P])
            dve.tensor_tensor(YE[:, e % 2, :].rearrange("p (t c) -> p t c", t=4),
                              bank[3 + e % 2][:, :].rearrange("p (t c) -> p t c", t=4), oh,
                              ALU.mult).then_inc(S["ye_masked"], 1)

        def pool_e_add(pool, b, e):
            pool.wait_ge(S["ye_masked"], b.n * NE + e + 1)
            if e == 0:
                pool.wait_ge(S["e_acc"], b.n + 1)
            else:
                pool.wait_ge(S["ye_added"], b.n * NE + e)
            settle(pool)
            pool.tensor_tensor(X[:, e_cols(b)], X[:, e_cols(b)], YE[:, e % 2, :], ALU.add).then_inc(S["ye_added"], 1)

        def sp_out(sp, b):
            sp.wait_ge(S["ye_added"], (b.n + 1) * NE)
            sp.dma_start(out[bass.ds(b.x * 2 * T, 2 * T), :].rearrange("(t p) c -> p t c", p=P),
                         X[:, e_cols(b)].rearrange("p (t c) -> p t c", c=C)).then_inc(S["out_done"], 16)

        def expert_slot(part, eng, pre, b):
            def do(step, x, e=0):
                if x is not None:
                    part(eng, step, x, e)
            do("stats", pre)
            do("hid", b, 0)
            do("norm", pre)
            do("hid", b, 1)
            do("T", pre)
            do("y", b, 0)
            do("gate", pre)
            do("hid", b, 2)
            do("y", b, 1)
            do("hid", b, 3)
            do("y", b, 2)
            do("y", b, 3)
            do("out", b)

        def experts(eng, part, layer):
            def slot(it, c):
                at = lambda d: None if it is None and not 0 <= c - d < NU else batch(layer, it, c - d, 2, NU)
                expert_slot(part, eng, at(0), at(1))
            slot(None, 0)
            slot(None, 1)
            with eng.Fori(0, NU // 2 - 1) as it:
                slot(it, 2)
                slot(it, 3)
            slot(None, NU)

        last_e = layers.count("F") - 1

        def dve_e_part(dve, step, b, e):
            if step == "stats":
                dve_e_stats(dve, b)
            elif step == "norm":
                dve_e_norm(dve, b)
            elif step == "gate":
                dve_e_route(dve, b)
            elif step == "hid":
                e_evac(dve, b, e, 1)
            elif step == "y":
                dve_e_mask(dve, b, e)

        def act_e_part(act, step, b, e):
            if step == "T":
                act_e_hT(act, b)
            elif step == "hid":
                e_evac(act, b, e, 0)

        def pool_e_part(pool, step, b, e):
            if step == "stats":
                pool_e_rstd(pool, b)
            elif step == "y":
                pool_e_add(pool, b, e)

        def pe_e_part(pe, step, b, e):
            if step == "T":
                pe_e_T(pe, b)
            elif step == "gate":
                pe_e_gate(pe, b)
            elif step == "hid":
                pe_e_hid(pe, b, e)
            elif step == "y":
                pe_e_y(pe, b, e)

        def sp_e_part(sp, step, b, e):
            if step == "out" and b.layer == last_e and layers[-1] == "F":
                sp_out(sp, b)

        AD = sb("AD", [P, 2, NT * MH])
        dts = sb("dts", [P, 10, NT * MH])
        YN = sb("YN", [P, NT, DI])
        f32 = lambda t: t[:, :].bitcast(F32)
        SZ = f32(k_tiles[0]).rearrange("p (m t c) -> p m t c", m=2, t=NT)
        XD = f32(k_tiles[1])[:, 0:2 * NT * DI].rearrange("p (m t c) -> p m t c", m=2, t=NT)
        GM = f32(k_tiles[1])[:, 2 * NT * DI:2 * NT * DI + 6 * P].rearrange("p (m c) -> p m c", m=2)
        R0, R1 = f32(q_tiles[0])[:, 0:MH * T], f32(q_tiles[0])[:, MH * T:MH * (T + P)]
        L0, L1 = f32(q_tiles[1])[:, 0:MH * T], f32(q_tiles[1])[:, MH * T:MH * (T + P)]
        PRF = PR[:, :, :].rearrange("p a t -> p (a t)")
        M0, M1 = PRF[:, 0:MH * T], PRF[:, MH * T:MH * (T + P)]
        EZ = roped
        EB = rest[0:DS, :, :].rearrange("p a t -> p (a t)")
        BCS, BSIN = YE[0:DS, 0, :], YE[0:DS, 1, :]
        BCR, BCOS = QKVG[0:DS, 0:2 * T], QKVG[0:DS, 2 * T:4 * T]
        Y3 = RT[:, 0:2, :]
        YNT = parts[:, :, :, :].rearrange("p a b t -> p (a b t)").bitcast(F32)[:, 0:2 * T]
        DT, DT_STEPS = 9, 18
        for n in """s_bn s_moments s_rstd s_normed s_xT s_hT s_zx s_bc s_dt_ready s_eb s_ez s_dt s_u
                    s_bcs s_rot s_bcr s_bcos s_g s_gm s_silu s_xd s_r s_seg s_l s_m s_y s_ysum s_ybn s_ymoments
                    s_yr s_yn s_yT s_yTe s_out s_resid_added""".split():
            S[n] = sem(n)

        def dve_s_stats(dve, b):
            wait(dve, S["s_normed"], b.n * 5)
            for t in range(NT):
                dve.bn_stats(st[:, t, :], X[:, xtile(b, t)]).then_inc(S["s_bn"], 1)
            dve.wait_ge(S["s_bn"], b.n * 2 + 2)
            settle(dve)
            for t in range(NT):
                dve.bn_aggr(mv[:, t, :], st[:, t, :]).then_inc(S["s_moments"], 1)

        def pool_s_rstd(pool, b):
            pool.wait_ge(S["s_moments"], b.n * 2 + 2)
            rstd_chain(pool, S["s_rstd"], b.n * 7, mv[:, 0:2, 1], rs, 2, True)

        def dve_s_norm(dve, b):
            dve.wait_ge(S["s_rstd"], b.n * 7 + 7)
            wait(dve, S["s_xT"], b.n)
            for r, o in ((6, 0), (1, NT)):
                for t in range(NT):
                    dve.tensor_scalar(XN[:, (o + t) * P:(o + t + 1) * P], X[:, xtile(b, t)], mv[:, t, 0:1],
                                      rs[:, r, t:t + 1], ALU.subtract, ALU.mult).then_inc(S["s_normed"], 1)
            dve.wait_ge(S["s_normed"], b.n * 5 + 4)
            dve.tensor_tensor(X[:, xcols(b)], X[:, xcols(b)], XN[:, NT * P:2 * NT * P],
                              ALU.add).then_inc(S["s_normed"], 1)

        def pe_s_T(pe, b):
            pe.wait_ge(S["s_normed"], b.n * 5 + 2)
            wait(pe, S["s_hT"], b.n)
            wait(pe, S["s_dt"], b.n * DT_STEPS - DT_STEPS + 1)
            for t in range(NT):
                mm = pe.transpose(bank[6][:, t * P:(t + 1) * P], XN[:, t * P:(t + 1) * P], ident[:, :])
            mm.then_inc(S["s_xT"], 1)

        def act_s_hT(act, b):
            act.wait_ge(S["s_xT"], b.n + 1)
            wait(act, S["s_dt_ready"], b.n)
            act.activation(HT[:, 0, 0:T], bank[6][:, 0:T], ACT.Identity, scale=W["cols"][:, 2:3],
                           bias=W["cols"][:, 3:4]).then_inc(S["s_hT"], 1)

        def pe_s_proj(pe, b):
            pe.wait_ge(S["s_hT"], b.n + 1)
            for t in range(NT):
                mm = pe.matmul(bank[6][:, T + t * MH:T + (t + 1) * MH], HT[:, 0, t * P:(t + 1) * P],
                               W["s_win"][:, 2 * DI + 2 * DS:], start=True, stop=True)
            mm.then_inc(S["s_dt_ready"], 1)
            wait(pe, S["s_bcs"], b.n)
            for i in range(2):
                mm = pe.matmul(bank[2][0:DS, i * T:(i + 1) * T],
                               W["s_win"][:, 2 * DI + i * DS:2 * DI + (i + 1) * DS], HT[:, 0, 0:T],
                               start=True, stop=True)
            mm.then_inc(S["s_bc"], 1)
            wait(pe, S["s_silu"], b.n * 2)
            for t in range(NT):
                pe.matmul(bank[t][:, :], HT[:, 0, t * P:(t + 1) * P], W["s_win"][:, 0:2 * DI],
                          start=True, stop=True).then_inc(S["s_zx"], 1)

        def act_s_exps(act, b):
            act.wait_ge(S["s_bc"], b.n + 1)
            wait(act, S["s_bcs"], b.n)
            act.activation(EB, bank[2][0:DS, :], ACT.Tanh, scale=0.5).then_inc(S["s_eb"], 1)
            wait(act, S["s_silu"], b.n * 2)
            for t in range(NT):
                act.wait_ge(S["s_zx"], b.n * 2 + t + 1)
                act.activation(EZ[:, t, :], bank[t][:, :], ACT.Tanh, scale=0.5).then_inc(S["s_ez"], 1)

        def dve_s_bc(dve, b):
            dve.wait_ge(S["s_eb"], b.n + 1)
            wait(dve, S["s_bcr"], b.n * 2)
            dve.scalar_tensor_tensor(BCS, EB, 1.0, bank[2][0:DS, :], ALU.add, ALU.mult).then_inc(S["s_bcs"], 1)

        def pe_s_rot(pe, b):
            pe.wait_ge(S["s_bcs"], b.n + 1)
            wait(pe, S["s_gm"], b.n)
            settle(pe)
            pe.matmul(bank[7][0:DS, :], W["c_turn"][:, :], BCS, start=True, stop=True).then_inc(S["s_rot"], 1)

        def pool_s_cos(pool, b):
            pool.wait_ge(S["s_bcs"], b.n + 1)
            wait(pool, S["s_bcr"], b.n * 2)
            settle(pool)
            pool.tensor_tensor(BCOS, BCS, W["c_rope_s"][:, 0:2 * T], ALU.mult).then_inc(S["s_bcos"], 1)

        def dve_s_rope(dve, b):
            dve.wait_ge(S["s_rot"], b.n + 1)
            dve.tensor_tensor(BSIN, bank[7][0:DS, :], W["c_rope_s"][:, 2 * T:], ALU.mult).then_inc(S["s_bcr"], 1)
            dve.wait_ge(S["s_bcos"], b.n + 1)
            dve.wait_ge(S["s_bcr"], b.n * 2 + 1)
            wait(dve, S["s_g"], b.n)
            dve.tensor_tensor(BCR, BSIN, BCOS, ALU.add).then_inc(S["s_bcr"], 1)

        def pe_s_g(pe, b):
            pe.wait_ge(S["s_bcr"], b.n * 2 + 2)
            pe.matmul(bank[7][:, 0:T], BCR[:, 0:P], BCR[:, T:2 * T], start=True, stop=True)
            pe.matmul(bank[7][:, T:T + P], BCR[:, P:T], BCR[:, T + P:2 * T], start=True,
                      stop=True).then_inc(S["s_g"], 1)

        def dve_s_gm(dve, b):
            dve.wait_ge(S["s_g"], b.n + 1)
            wait(dve, S["s_m"], done(b, 2, 2))
            dve.tensor_tensor(GM[:, b.m, :], bank[7][:, 0:3 * P], W["c_upto16"][:, :], ALU.mult).then_inc(S["s_gm"], 1)

        def dve_s_dt(dve, b, second):
            s, v = S["s_dt"], b.n * DT_STEPS
            x, neg, mag, u, den, ratio, sq, poly, pos, dt = (dts[:, k, :] for k in range(10))

            def step(k, ins):
                ins.then_inc(s, 1)
                dve.wait_ge(s, v + k)
            if not second:
                dve.wait_ge(S["s_dt_ready"], b.n + 1)
                wait(dve, S["s_xd"], b.n * 4)
                step(1, dve.tensor_tensor(x, bank[6][:, T:T + NT * MH], W["rows"][:, 16:24], ALU.add))
                step(2, dve.tensor_scalar(neg, x, -1.0, None, ALU.mult))
                step(3, dve.tensor_tensor(mag, x, neg, ALU.max))
                return
            dve.wait_ge(S["s_u"], b.n + 1)
            step(4, dve.tensor_scalar(den, u, 2.0, None, ALU.add))
            step(5, dve.reciprocal(den, den))
            step(6, dve.tensor_tensor(ratio, u, den, ALU.mult))
            step(7, dve.tensor_tensor(sq, ratio, ratio, ALU.mult))
            step(8, dve.tensor_scalar(poly, sq, 1.0 / 15, None, ALU.mult))
            for k in range(6):
                step(9 + k, dve.scalar_tensor_tensor(poly, poly, 1.0 / (13 - 2 * k), sq, ALU.add, ALU.mult))
            step(15, dve.scalar_tensor_tensor(poly, poly, 1.0, ratio, ALU.add, ALU.mult))
            step(16, dve.tensor_scalar(pos, x, 0.0, None, ALU.max))
            step(17, dve.scalar_tensor_tensor(dt, poly, 2.0, pos, ALU.mult, ALU.add))
            wait(dve, S["s_r"], done(b, 2, 2))
            step(18, dve.tensor_tensor(AD[:, b.m, :].rearrange("p (t h) -> p t h", t=NT),
                                       dt.rearrange("p (t h) -> p t h", t=NT),
                                       a_neg[:, :].unsqueeze(1).broadcast_to([P, NT, MH]), ALU.mult))

        def act_s_dt(act, b):
            act.wait_ge(S["s_dt"], b.n * DT_STEPS + 3)
            act.activation(dts[:, 3, :], dts[:, 2, :], ACT.Exp, scale=-1.0).then_inc(S["s_u"], 1)

        def dve_s_silu(dve, b, t):
            dve.wait_ge(S["s_ez"], b.n * 2 + t + 1)
            if t == 0:
                wait(dve, S["s_ysum"], done(b, 2, 4))
            dve.scalar_tensor_tensor(SZ[:, b.m, t, :], EZ[:, t, :], 1.0, bank[t][:, :], ALU.add,
                                     ALU.mult).then_inc(S["s_silu"], 1)

        def pool_s_xd(pool, b):
            pool.wait_ge(S["s_silu"], b.n * 2 + 2)
            pool.wait_ge(S["s_dt"], b.n * DT_STEPS + 17)
            wait(pool, S["s_y"], done(b, 2, 1))
            heads = lambda ap: ap.rearrange("p (h c) -> p h c", h=MH)
            for t in range(NT):
                dt = dts[:, DT, t * MH:(t + 1) * MH].unsqueeze(2).broadcast_to([P, MH, MP])
                settle(pool)
                pool.tensor_tensor(heads(XD[:, b.m, t, :]), heads(SZ[:, b.m, t, DI:]), dt,
                                   ALU.mult).then_inc(S["s_xd"], 1)
            pool.wait_ge(S["s_xd"], b.n * 4 + 2)
            for t in range(NT):
                dd = d_quarter[:, :].unsqueeze(2).broadcast_to([P, MH, MP])
                settle(pool)
                pool.tensor_tensor(heads(SZ[:, b.m, t, DI:]), heads(SZ[:, b.m, t, DI:]), dd,
                                   ALU.mult).then_inc(S["s_xd"], 1)

        def pool_s_r(pool, b):
            pool.wait_ge(S["s_dt"], b.n * DT_STEPS + 18)
            wait(pool, S["s_seg"], b.n * 3)
            for dst, t, cols, n in ((R0, 0, slice(0, T), T), (R1, 1, slice(T, T + P), P)):
                settle(pool)
                pool.tensor_tensor(dst.rearrange("p (h t) -> p h t", h=MH),
                                   W["c_upto"][:, cols].unsqueeze(1).broadcast_to([P, MH, n]),
                                   AD[:, b.m, t * MH:(t + 1) * MH].unsqueeze(2).broadcast_to([P, MH, n]),
                                   ALU.mult).then_inc(S["s_r"], 1)

        def pe_s_seg(pe, b):
            pe.wait_ge(S["s_r"], b.n * 2 + 2)
            wait(pe, S["s_ysum"], b.n * 4)
            for i in range(2):
                bk = bank[3 + i]
                pe.matmul(bk[:, :], W["c_after"][:, :], R0[:, i * 2 * T:(i + 1) * 2 * T], start=True, stop=False,
                          skip_group_check=True)
                pe.matmul(bk[:, :].rearrange("p (h t) -> p h t", h=2)[:, :, P:T], ones[:, :],
                          R1[:, i * 2 * P:(i + 1) * 2 * P], start=False, stop=True,
                          skip_group_check=True).then_inc(S["s_seg"], 1)
            wait(pe, S["s_resid_added"], done(b, 2, 1))
            pe.matmul(bank[5][:, :], W["c_after"][:, :], R1, start=True, stop=True).then_inc(S["s_seg"], 1)

        def act_s_l(act, b):
            wait(act, S["s_m"], b.n * 2)
            for i, dst in enumerate((L0[:, 0:2 * T], L0[:, 2 * T:4 * T], L1)):
                act.wait_ge(S["s_seg"], b.n * 3 + i + 1)
                act.activation(dst, bank[3 + i][:, :], ACT.Exp).then_inc(S["s_l"], 1)

        def dve_s_m(dve, b):
            dve.wait_ge(S["s_l"], b.n * 3 + 3)
            dve.wait_ge(S["s_gm"], b.n + 1)
            wait(dve, S["s_y"], b.n)
            for dst, src, cols, n in ((M0, L0, slice(0, T), T), (M1, L1, slice(T, T + P), P)):
                heads = lambda ap: ap.rearrange("p (h t) -> p h t", h=MH)
                dve.tensor_tensor(heads(dst), heads(src), GM[:, b.m, cols].unsqueeze(1).broadcast_to([P, MH, n]),
                                  ALU.mult).then_inc(S["s_m"], 1)

        def pe_s_y(pe, b):
            pe.wait_ge(S["s_m"], b.n * 2 + 2)
            pe.wait_ge(S["s_xd"], b.n * 4 + 2)
            for h in range(MH):
                pe.matmul(bank[3][:, h * MP:(h + 1) * MP], M0[:, h * T:h * T + P], XD[:, b.m, 0, h * MP:(h + 1) * MP],
                          start=(h == 0), stop=True, skip_group_check=True)
            for h in range(MH):
                dst = bank[4][:, h * MP:(h + 1) * MP]
                pe.matmul(dst, M0[:, h * T + P:(h + 1) * T], XD[:, b.m, 0, h * MP:(h + 1) * MP],
                          start=(h == 0), stop=False, skip_group_check=True)
                mm = pe.matmul(dst, M1[:, h * P:(h + 1) * P], XD[:, b.m, 1, h * MP:(h + 1) * MP],
                               start=False, stop=True, skip_group_check=True)
            mm.then_inc(S["s_y"], 1)

        def dve_s_gate(dve, b):
            dve.wait_ge(S["s_y"], b.n + 1)
            dve.wait_ge(S["s_xd"], b.n * 4 + 4)
            wait(dve, S["s_yn"], b.n * 2)
            for t in range(NT):
                dve.tensor_tensor(Y3[:, t, :], bank[3 + t][:, 0:DI], SZ[:, b.m, t, DI:], ALU.add).then_inc(S["s_ysum"], 1)
            dve.wait_ge(S["s_ysum"], b.n * 4 + 2)
            for t in range(NT):
                dve.tensor_tensor(Y3[:, t, :], Y3[:, t, :], SZ[:, b.m, t, 0:DI], ALU.mult).then_inc(S["s_ysum"], 1)
            dve.wait_ge(S["s_ysum"], b.n * 4 + 4)
            for t in range(NT):
                dve.bn_stats(lst[:, t, :], Y3[:, t, :]).then_inc(S["s_ybn"], 1)
            dve.wait_ge(S["s_ybn"], b.n * 2 + 2)
            wait(dve, S["s_yr"], b.n * 4)
            settle(dve)
            for t in range(NT):
                dve.bn_aggr(lmv[:, t, :], lst[:, t, :]).then_inc(S["s_ymoments"], 1)

        def pool_s_yr(pool, b):
            s, v = S["s_yr"], b.n * 4
            pool.wait_ge(S["s_ymoments"], b.n * 2 + 2)
            wait(pool, S["s_yn"], b.n * 2)
            settle(pool)
            pool.tensor_tensor(yrs[:, 0, :], lmv[:, :, 0], lmv[:, :, 0], ALU.mult).then_inc(s, 1)
            pool.wait_ge(s, v + 1)
            settle(pool)
            pool.tensor_tensor(yrs[:, 1, :], yrs[:, 0, :], lmv[:, :, 1], ALU.add).then_inc(s, 1)
            pool.wait_ge(s, v + 2)
            settle(pool)
            pool.tensor_scalar(yrs[:, 2, :], yrs[:, 1, :], 1e-6, None, ALU.add).then_inc(s, 1)
            pool.wait_ge(s, v + 3)
            settle(pool)
            pool.tensor_tensor(yrs[:, 3, :], yrs[:, 2, :], power[:, 0:2], ALU.pow).then_inc(s, 1)

        def dve_s_yn(dve, b):
            dve.wait_ge(S["s_yr"], b.n * 4 + 4)
            wait(dve, S["s_yT"], b.n)
            for t in range(NT):
                dve.tensor_scalar(YN[:, t, :], Y3[:, t, :], yrs[:, 3, t:t + 1], None, ALU.mult).then_inc(S["s_yn"], 1)

        def pe_s_yT(pe, b):
            pe.wait_ge(S["s_yn"], b.n * 2 + 2)
            pe.wait_ge(S["s_l"], min2(b.n + 2, NB) * 3)
            for half in range(2):
                for t in range(NT):
                    mm = pe.transpose(bank[5][:, half * T + t * P:half * T + (t + 1) * P],
                                      YN[:, t, half * P:(half + 1) * P], ident[:, :])
            mm.then_inc(S["s_yT"], 1)

        def act_s_yT(act, b):
            act.wait_ge(S["s_yT"], b.n + 1)
            wait(act, S["s_out"], b.n)
            for half in range(2):
                act.activation(YNT[:, half * T:(half + 1) * T], bank[5][:, half * T:(half + 1) * T], ACT.Identity,
                               scale=W["cols"][:, 4 + half:5 + half]).then_inc(S["s_yTe"], 1)

        def pe_s_out(pe, b):
            pe.wait_ge(S["s_yTe"], b.n * 2 + 2)
            for t in range(NT):
                for half in range(2):
                    mm = pe.matmul(bank[5][:, t * P:(t + 1) * P], YNT[:, half * T + t * P:half * T + (t + 1) * P],
                                   W["s_wout"][:, half * P:(half + 1) * P], start=(t == 0 and half == 0),
                                   stop=(half == 1), skip_group_check=True)
            mm.then_inc(S["s_out"], 1)

        def dve_s_resid(dve, b):
            dve.wait_ge(S["s_out"], b.n + 1)
            dve.tensor_tensor(X[:, xcols(b)], X[:, xcols(b)], bank[5][:, 0:T], ALU.add).then_inc(S["s_resid_added"], 1)

        yrs = sb("yrs", [P, 4, 2])

        MIXER_ORDER = (("seg", 2), ("yn", 3), ("stats", 0), ("bc", 1), ("dt", 1), ("silu", 1), ("y_T", 3),
                       ("mul", 2), ("norm", 0), ("rope", 1), ("out", 3), ("dt2", 1), ("gate", 2), ("proj", 0),
                       ("gm", 1), ("exps", 0), ("resid", 3), ("xd", 1))

        def mixer(eng, part):
            def slot(it, c):
                for step, d in MIXER_ORDER:
                    if it is not None or 0 <= c - d < NB:
                        part(eng, step, batch(0, it, c - d, 2))
            for c in range(4):
                slot(None, c)
            with eng.Fori(0, (NB - 4) // 2) as it:
                slot(it, 4)
                slot(it, 5)
            for c in range(NB, NB + 3):
                slot(None, c)

        def dve_s_part(dve, step, b):
            if step == "stats":
                dve_s_stats(dve, b)
            elif step == "norm":
                dve_s_norm(dve, b)
            elif step == "dt":
                dve_s_dt(dve, b, False)
            elif step == "dt2":
                dve_s_dt(dve, b, True)
            elif step == "mul":
                dve_s_m(dve, b)
            elif step == "gate":
                dve_s_gate(dve, b)
            elif step == "bc":
                dve_s_bc(dve, b)
            elif step == "yn":
                dve_s_yn(dve, b)
            elif step == "rope":
                dve_s_rope(dve, b)
            elif step == "gm":
                dve_s_gm(dve, b)
            elif step == "silu":
                dve_s_silu(dve, b, 0)
                dve_s_silu(dve, b, 1)
            elif step == "resid":
                dve_s_resid(dve, b)

        def pool_s_part(pool, step, b):
            if step == "stats":
                pool_s_rstd(pool, b)
            elif step == "bc":
                pool_s_cos(pool, b)
            elif step == "dt2":
                pool_s_r(pool, b)
            elif step == "gate":
                pool_s_yr(pool, b)
            elif step == "xd":
                pool_s_xd(pool, b)

        def act_s_part(act, step, b):
            if step == "norm":
                act_s_hT(act, b)
            elif step == "seg":
                act_s_l(act, b)
            elif step == "exps":
                act_s_exps(act, b)
            elif step == "dt":
                act_s_dt(act, b)
            elif step == "y_T":
                act_s_yT(act, b)

        def pe_s_part(pe, step, b):
            if step == "norm":
                pe_s_T(pe, b)
            elif step == "proj":
                pe_s_proj(pe, b)
            elif step == "seg":
                pe_s_seg(pe, b)
            elif step == "mul":
                pe_s_y(pe, b)
            elif step == "bc":
                pe_s_rot(pe, b)
            elif step == "rope":
                pe_s_g(pe, b)
            elif step == "y_T":
                pe_s_yT(pe, b)
            elif step == "out":
                pe_s_out(pe, b)

        def sp_s_part(sp, step, b):
            pass

        def before(eng, i):
            if i == 0:
                eng.wait_ge(S["early_loaded"], 16 * len(EARLY))
                eng.wait_ge(S["x_loaded"], 16)
                eng.wait_ge(S["const_set"], 4)
                eng.wait_ge(S["ones_rows"], 3)
                eng.wait_ge(S["v_ones"], 3)
                eng.wait_ge(S["bias_split"], 10)
                return
            kind = layers[i - 1]
            if kind == "S":
                eng.wait_ge(S["s_resid_added"], NB)
                if eng is nc.gpsimd:
                    ones_rows(eng, 3)
                if i < len(layers):
                    eng.wait_ge(S["ones_rows"], 6)
            elif kind == "F":
                eng.wait_ge(S["ye_added"], layers[:i].count("F") * NU * NE)
            else:
                eng.wait_ge(S["resid_added"], NB)

        def ones_rows(eng, n):
            for i in range(3):
                eng.memset(k_tiles[i][64:96, :], 1.0).then_inc(S["ones_rows"], 1)
                eng.wait_ge(S["ones_rows"], n + i + 1)

        def run(eng, att, exp, mix):
            f = 0
            for i, kind in enumerate(layers):
                if kind != "F" or layers[i - 1] != "A":
                    before(eng, i)
                if kind == "A":
                    attention(eng, att, 0)
                elif kind == "F":
                    attention(eng, att, f + 1)
                    eng.wait_ge(S["resid_added"], (f + 2) * NB)
                    experts(eng, exp, f)
                    f += 1
                else:
                    mixer(eng, mix)

        block = ctx.enter_context(nc.Block())

        @block.sync
        def _(sp):
            def load_x(lo, hi, loaded):
                sp.dma_start(X[:, lo * T:hi * T].rearrange("p (t c) -> p t c", c=C),
                             x_in[lo:hi].rearrange("b (t p) c -> p (b t) c", p=P)).then_inc(loaded, 16)

            def load(k, loaded):
                v = w[k]
                if k in ("bias_rows", "rows"):
                    v = v.broadcast_to([W[k].shape[0], v.shape[1]])
                sp.dma_start(W[k][:, :], v).then_inc(loaded, 16)
            load_x(0, FIRST_LOAD, S["x_loaded"])
            for k in EARLY:
                load(k, S["early_loaded"])
            load_x(FIRST_LOAD, NB, S["x_rest_loaded"])
            for k in w:
                if k not in EARLY:
                    load(k, S["rest_loaded"])
            run(sp, sp_part, sp_e_part, sp_s_part)
            if layers[-1] == "F":
                sp.wait_ge(S["out_done"], 16 * NU)
            else:
                before(sp, len(layers))
                sp.dma_start(out.rearrange("(t p) c -> p t c", p=P),
                             X[:, :].rearrange("p (t c) -> p t c", c=C)).then_inc(S["out_done"], 16)
                sp.wait_ge(S["out_done"], 16)

        @block.gpsimd
        def _(pool):
            for i in range(3):
                pool.memset(VP[i][:, :].rearrange("p (m c) -> p m c", c=VPITCH)[:, :, 3 * HD:], 1.0).then_inc(S["v_ones"], 1)
            pool.memset(exp_shift[:, :], EXP_SHIFT).then_inc(S["const_set"], 1)
            pool.memset(ones3[:, :], 1.0).then_inc(S["const_set"], 1)
            pool.memset(ones[:, :], 1.0).then_inc(S["const_set"], 1)
            pool.memset(power[:, :], -0.5).then_inc(S["const_set"], 1)
            pool.wait_ge(S["v_ones"], 3)
            pool.wait_ge(S["const_set"], 4)
            ones_rows(pool, 0)
            run(pool, pool_part, pool_e_part, pool_s_part)

        @block.vector
        def _(dve):
            s = S["bias_split"]
            dve.wait_ge(S["early_loaded"], 16 * len(EARLY))
            dve.tensor_copy(bias_hi, W["bias_rows"][:, :]).then_inc(s, 1)
            dve.wait_ge(s, 1)
            dve.tensor_scalar(bias_r, bias_hi, W["c_part"][:, 0:1], None, ALU.mult).then_inc(s, 1)
            dve.wait_ge(s, 2)
            dve.tensor_tensor(bias_r, W["bias_rows"][:, :], bias_r, ALU.subtract).then_inc(s, 1)
            dve.wait_ge(s, 3)
            dve.tensor_copy(bias_mid, bias_r).then_inc(s, 1)
            dve.wait_ge(s, 4)
            dve.tensor_scalar(bias_parts[:, :], bias_mid, W["c_part"][:, 1:2], None, ALU.mult).then_inc(s, 1)
            dve.wait_ge(s, 5)
            dve.tensor_tensor(bias_parts[:, :], bias_r, bias_parts[:, :], ALU.subtract).then_inc(s, 1)
            dve.wait_ge(s, 6)
            dve.tensor_copy(b2_rows[:, :].rearrange("p (e t c) -> p e t c", e=NE, t=4),
                            bias_parts[:, 0:NE * C].rearrange("p (e c) -> p e c", e=NE).unsqueeze(2)
                            .broadcast_to([3, NE, 4, C])).then_inc(s, 1)
            dve.wait_ge(s, 8)
            dve.tensor_scalar(a_neg[:, :], a_neg[:, :], -1.0, None, ALU.mult).then_inc(s, 1)
            dve.tensor_scalar(d_quarter[:, :], W["rows"][:, 28:32], 0.25, None, ALU.mult).then_inc(s, 1)
            run(dve, dve_part, dve_e_part, dve_s_part)

        @block.scalar
        def _(act):
            act.wait_ge(S["early_loaded"], 16 * len(EARLY))
            act.wait_ge(S["bias_split"], 7)
            act.activation(a_neg[:, :], W["rows"][:, 24:28], ACT.Exp).then_inc(S["bias_split"], 1)
            run(act, act_part, act_e_part, act_s_part)

        @block.tensor
        def _(pe):
            run(pe, pe_part, pe_e_part, pe_s_part)


LAYERS = "AFSF"


def kernel(**inputs):
    import concourse.bacc as bacc
    from concourse.bass_utils import run_bass_kernel_spmd as launch

    a = {k: np.asarray(v) for k, v in inputs.items()}
    nc = bacc.Bacc("TRN2", target_bir_lowering=False, num_devices=1)
    arrays = {"x": np.ascontiguousarray(a["L0_attn_a_x"])}
    arrays.update(layouts(a))
    arrays.update(constants())
    aps = {k: nc.dram_tensor(k, v.shape, mybir.dt.from_np(v.dtype), kind="ExternalInput").ap()
           for k, v in arrays.items()}
    out = nc.dram_tensor("out", (NB * T, C), F32, kind="ExternalOutput").ap()
    x_ap = aps.pop("x")
    program(nc, x_ap, aps, out, LAYERS)
    r = launch(nc, [arrays], core_ids=[0])
    return np.asarray(r.results[0]["out"]).reshape(NB, T, C)
```
